# Optimizing a Trainium2 kernel written in Bass

```python
import numpy as np
import jax
import jax.numpy as jnp

def _softmax(x, axis=-1):
    return jax.nn.softmax(x, axis=axis)

def _gelu(x):
    return jax.nn.gelu(x, approximate=True)

def _silu(x):
    return jax.nn.silu(x)

def _sigmoid(x):
    return jax.nn.sigmoid(x)

def _layernorm(x, axis=-1, eps=1e-05):
    m = jnp.mean(x, axis=axis, keepdims=True)
    v = jnp.var(x, axis=axis, keepdims=True)
    return (x - m) / jnp.sqrt(v + eps)

def _scatter_add(tgt, idx, src, axis=0):
    return tgt.at[idx].add(src)

def _segment_sum(src, seg, n):
    return jax.ops.segment_sum(src, seg, n)
kernel_name = 'mk_flamingo_gated_d2_seqx_r8_682f0c'

def setup_inputs(seed: int=0):
    np.random.seed(seed)
    _w = jnp.asarray

    def _rec_inputs():
        import jax
        import jax.numpy as jnp
        _rk = jax.random.key(seed)
        x = -0.0003929 + 0.9999 * jax.random.normal(jax.random.fold_in(_rk, 1), (8, 128, 256), jnp.float32)
        _lenS = 128 - jax.random.randint(jax.random.fold_in(_rk, 7), (8,), 0, max(1, 128 // 4) + 1, jnp.int32)
        _lenS2 = 128 - jax.random.randint(jax.random.fold_in(_rk, 8), (8,), 0, max(1, 128 // 4) + 1, jnp.int32)
        _ctx_2048P = jax.random.normal(jax.random.fold_in(_rk, 11), (8, 16, 256), jnp.float32)
        _ctx_2048c = jax.random.dirichlet(jax.random.fold_in(_rk, 511), 0.3 * jnp.ones((16,), jnp.float32), (8, 128))
        _ctx_2048t = jnp.einsum('bsk,bkd->bsd', _ctx_2048c, _ctx_2048P)
        _ctx_2048t = _ctx_2048t * jax.lax.rsqrt(jnp.mean(jnp.square(_ctx_2048t)) + 1e-12) * 0.953939
        ctx_2048 = 2.81802e-05 + 1.00001 * (_ctx_2048t + 0.3 * jax.random.normal(jax.random.fold_in(_rk, 611), (8, 128, 256), jnp.float32))
        _g = jax.random.normal(jax.random.fold_in(_rk, 9001), (2, 2), jnp.float32)
        _g = jnp.sign(_g) * jnp.maximum(jnp.abs(_g), 1.0) + (_g == 0) * 1.0
        g_xattn = _g[0]
        g_ffn = _g[1]
        return (x, ctx_2048, g_xattn, g_ffn)
    x, ctx_2048, g_xattn, g_ffn = _rec_inputs()

    def _L0_xattn_setup():
        import jax, jax.numpy as jnp
        import numpy as np
        HIDDEN = 256
        NUM_HEADS = 16
        HEAD_DIM = HIDDEN // NUM_HEADS
        CHUNK = 128
        SCALE = HEAD_DIM ** (-0.5)

        def _chunked_causal_attention(q, k, v):
            B, H, S, D = q.shape
            n_chunks = S // CHUNK
            kc = k.reshape(B, H, n_chunks, CHUNK, D).transpose(2, 0, 1, 3, 4)
            vc = v.reshape(B, H, n_chunks, CHUNK, D).transpose(2, 0, 1, 3, 4)
            j0s = jnp.arange(n_chunks) * CHUNK
            q_idx = jnp.arange(S)[:, None]
            k_off = jnp.arange(CHUNK)[None, :]
            out0 = jnp.zeros_like(q)
            m0 = jnp.full((B, H, S, 1), -jnp.inf, dtype=q.dtype)
            s0 = jnp.zeros((B, H, S, 1), dtype=q.dtype)

            def step(carry, inputs):
                out, m, s = carry
                kj, vj, j0 = inputs
                scores = jnp.einsum('bhqd,bhkd->bhqk', q, kj) * SCALE
                causal = j0 + k_off > q_idx
                scores = jnp.where(causal[None, None], -jnp.inf, scores)
                chunk_max = scores.max(axis=-1, keepdims=True)
                new_m = jnp.maximum(m, chunk_max)
                exp_old = jnp.exp(m - new_m)
                exp_c = jnp.exp(scores - new_m)
                new_s = s * exp_old + exp_c.sum(axis=-1, keepdims=True)
                out = out * (s / new_s) * exp_old + jnp.einsum('bhqk,bhkd->bhqd', exp_c / new_s, vj)
                return ((out, new_m, new_s), None)
            (out, _, _), _ = jax.lax.scan(step, (out0, m0, s0), (kc, vc, j0s))
            return out
        key = jax.random.key(seed)
        kq, kk, kv = jax.random.split(key, 3)
        B, S = (2, 512)
        return {'query': jax.random.normal(kq, (B, S, HIDDEN), dtype=jnp.float32), 'key': jax.random.normal(kk, (B, S, HIDDEN), dtype=jnp.float32), 'value': jax.random.normal(kv, (B, S, HIDDEN), dtype=jnp.float32)}
    _L0_xattn_all = _L0_xattn_setup()
    _L0_xattn_in = {k: v for k, v in _L0_xattn_all.items() if k in ()}
    del _L0_xattn_all

    def _L0_ffn_setup():
        import jax, jax.numpy as jnp
        import numpy as np
        R = 64
        RP = 2
        K = 8
        SCALING = 16.0 / K
        key = jax.random.key(seed)
        ks = jax.random.split(key, 5)
        B, S, Din, Dout = (8, 512, 256, 256)
        x = jax.random.normal(ks[0], (B, S, Din), dtype=jnp.float32)
        base_W = jax.random.normal(ks[1], (Dout, Din), dtype=jnp.float32) * Din ** (-0.5)
        router_W = jax.random.normal(ks[2], (R // RP, Din), dtype=jnp.float32) * Din ** (-0.5)
        A = jax.random.normal(ks[3], (R, Din), dtype=jnp.float32) * Din ** (-0.5)
        Bw = jax.random.normal(ks[4], (Dout, R), dtype=jnp.float32) * R ** (-0.5)
        biases = jnp.zeros((R,), dtype=jnp.float32)
        return {'x': x, 'base_W': base_W, 'router_W': router_W, 'A': A, 'B': Bw, 'biases': biases}
    _L0_ffn_all = _L0_ffn_setup()
    _L0_ffn_in = {k: v for k, v in _L0_ffn_all.items() if k in ('base_W', 'router_W', 'A', 'B', 'biases')}
    del _L0_ffn_all

    def _L1_xattn_setup():
        import jax, jax.numpy as jnp
        import numpy as np
        key = jax.random.key(seed)
        k1, k2, k3, k4, k5 = jax.random.split(key, 5)
        B, D_MODEL, L = (2, 128, 256)
        HEAD_DIM = 8
        H = D_MODEL // HEAD_DIM
        return {'k': jax.random.normal(k1, (B, D_MODEL, L), dtype=jnp.float32), 'v': jax.random.normal(k2, (B, D_MODEL, L), dtype=jnp.float32), 'q': jax.random.normal(k3, (B, D_MODEL, L), dtype=jnp.float32), 'ssm_kernel': jax.random.normal(k4, (H, L), dtype=jnp.float32), 'D': jax.random.normal(k5, (H,), dtype=jnp.float32), 'head_dim': HEAD_DIM}
    _L1_xattn_all = _L1_xattn_setup()
    _L1_xattn_in = {k: v for k, v in _L1_xattn_all.items() if k in ('ssm_kernel', 'D')}
    del _L1_xattn_all

    def _L1_ffn_setup():
        import jax, jax.numpy as jnp
        import numpy as np
        B, S, D = (4, 128, 256)
        H = 512
        NE = 8
        TOPK = 2
        key = jax.random.key(seed)
        ks = jax.random.split(key, 9)
        s = lambda fan_in: 1.0 / np.sqrt(fan_in)
        return {'x': jax.random.normal(ks[0], (B, S, D), dtype=jnp.float32), 'W1': jax.random.normal(ks[1], (NE, D, H), dtype=jnp.float32) * s(D), 'b1': jnp.zeros((NE, H), dtype=jnp.float32), 'W2': jax.random.normal(ks[2], (NE, H, H), dtype=jnp.float32) * s(H), 'b2': jnp.zeros((NE, H), dtype=jnp.float32), 'W3': jax.random.normal(ks[3], (NE, H, D), dtype=jnp.float32) * s(H), 'b3': jnp.zeros((NE, D), dtype=jnp.float32), 'Wg': jax.random.normal(ks[4], (D, NE), dtype=jnp.float32) * s(D), 'bg': jnp.zeros((NE,), dtype=jnp.float32)}
    _L1_ffn_all = _L1_ffn_setup()
    _L1_ffn_in = {k: v for k, v in _L1_ffn_all.items() if k in ('W1', 'b1', 'W2', 'b2', 'W3', 'b3', 'Wg', 'bg')}
    del _L1_ffn_all
    return {'x': x, 'ctx_2048': ctx_2048, 'g_xattn': g_xattn, 'g_ffn': g_ffn, 'L0_ffn_base_W': _L0_ffn_in['base_W'], 'L0_ffn_router_W': _L0_ffn_in['router_W'], 'L0_ffn_A': _L0_ffn_in['A'], 'L0_ffn_B': _L0_ffn_in['B'], 'L0_ffn_biases': _L0_ffn_in['biases'], 'L1_xattn_ssm_kernel': _L1_xattn_in['ssm_kernel'], 'L1_xattn_D': _L1_xattn_in['D'], 'L1_ffn_W1': _L1_ffn_in['W1'], 'L1_ffn_b1': _L1_ffn_in['b1'], 'L1_ffn_W2': _L1_ffn_in['W2'], 'L1_ffn_b2': _L1_ffn_in['b2'], 'L1_ffn_W3': _L1_ffn_in['W3'], 'L1_ffn_b3': _L1_ffn_in['b3'], 'L1_ffn_Wg': _L1_ffn_in['Wg'], 'L1_ffn_bg': _L1_ffn_in['bg']}

def reference(x, ctx_2048, g_xattn, g_ffn, L0_ffn_base_W, L0_ffn_router_W, L0_ffn_A, L0_ffn_B, L0_ffn_biases, L1_xattn_ssm_kernel, L1_xattn_D, L1_ffn_W1, L1_ffn_b1, L1_ffn_W2, L1_ffn_b2, L1_ffn_W3, L1_ffn_b3, L1_ffn_Wg, L1_ffn_bg):
    import jax
    import jax.numpy as jnp

    def _L0_xattn_ref(query, key, value):
        import jax, jax.numpy as jnp
        import numpy as np
        HIDDEN = 256
        NUM_HEADS = 16
        HEAD_DIM = HIDDEN // NUM_HEADS
        CHUNK = 128
        SCALE = HEAD_DIM ** (-0.5)

        def _chunked_causal_attention(q, k, v):
            B, H, S, D = q.shape
            n_chunks = S // CHUNK
            kc = k.reshape(B, H, n_chunks, CHUNK, D).transpose(2, 0, 1, 3, 4)
            vc = v.reshape(B, H, n_chunks, CHUNK, D).transpose(2, 0, 1, 3, 4)
            j0s = jnp.arange(n_chunks) * CHUNK
            q_idx = jnp.arange(S)[:, None]
            k_off = jnp.arange(CHUNK)[None, :]
            out0 = jnp.zeros_like(q)
            m0 = jnp.full((B, H, S, 1), -jnp.inf, dtype=q.dtype)
            s0 = jnp.zeros((B, H, S, 1), dtype=q.dtype)

            def step(carry, inputs):
                out, m, s = carry
                kj, vj, j0 = inputs
                scores = jnp.einsum('bhqd,bhkd->bhqk', q, kj) * SCALE
                causal = j0 + k_off > q_idx
                scores = jnp.where(causal[None, None], -jnp.inf, scores)
                chunk_max = scores.max(axis=-1, keepdims=True)
                new_m = jnp.maximum(m, chunk_max)
                exp_old = jnp.exp(m - new_m)
                exp_c = jnp.exp(scores - new_m)
                new_s = s * exp_old + exp_c.sum(axis=-1, keepdims=True)
                out = out * (s / new_s) * exp_old + jnp.einsum('bhqk,bhkd->bhqd', exp_c / new_s, vj)
                return ((out, new_m, new_s), None)
            (out, _, _), _ = jax.lax.scan(step, (out0, m0, s0), (kc, vc, j0s))
            return out
        B, S, _ = query.shape
        q = query.reshape(B, S, NUM_HEADS, HEAD_DIM).transpose(0, 2, 1, 3)
        k = key.reshape(B, S, NUM_HEADS, HEAD_DIM).transpose(0, 2, 1, 3)
        v = value.reshape(B, S, NUM_HEADS, HEAD_DIM).transpose(0, 2, 1, 3)
        out = _chunked_causal_attention(q, k, v)
        return out.transpose(0, 2, 1, 3).reshape(B, S, HIDDEN)

    def _L0_ffn_ref(x, base_W, router_W, A, B, biases):
        import jax, jax.numpy as jnp
        import numpy as np
        R = 64
        RP = 2
        K = 8
        SCALING = 16.0 / K
        Bsz, S, Din = x.shape
        N = Bsz * S
        xf = x.reshape(N, Din)
        logits = jax.nn.sigmoid(xf @ router_W.T)
        logits = jnp.repeat(logits, RP, axis=-1) + biases
        top_v, top_i = jax.lax.top_k(logits, K)
        rows = jnp.arange(N)[:, None]
        sparse = jnp.zeros((N, R), dtype=x.dtype).at[rows, top_i].set(top_v)
        gating = sparse / jnp.sum(sparse, axis=-1, keepdims=True) * K
        mid = xf @ A.T
        lora_out = mid * gating @ B.T
        base = xf @ base_W.T
        out = base + SCALING * lora_out
        return out.reshape(Bsz, S, -1)

    def _L1_xattn_ref(k, v, q, ssm_kernel, D, head_dim):
        import jax, jax.numpy as jnp
        import numpy as np
        B, HD, L = k.shape
        H = HD // head_dim
        fft_size = 2 * L
        k_ = k.reshape(B, H, head_dim, L)
        v_ = v.reshape(B, H, head_dim, L)
        q_ = q.reshape(B, H, head_dim, L)
        kv = jnp.einsum('bhil,bhjl->bijhl', k_, v_)
        kv_f = jnp.fft.rfft(kv, n=fft_size)
        kernel_f = jnp.fft.rfft(ssm_kernel, n=fft_size)
        y = jnp.fft.irfft(kv_f * kernel_f, n=fft_size)[..., :L]
        out = y + kv * D[None, None, None, :, None]
        out = jnp.einsum('bijhl,bhil->bjhl', out, q_)
        out = jnp.transpose(out, (0, 2, 1, 3)).reshape(B, H * head_dim, L)
        return out.astype(k.dtype)

    def _L1_ffn_ref(x, W1, b1, W2, b2, W3, b3, Wg, bg):
        import jax, jax.numpy as jnp
        import numpy as np
        B, S, D = (4, 128, 256)
        H = 512
        NE = 8
        TOPK = 2
        gate_logits = jnp.einsum('bsd,dn->bsn', x, Wg) + bg
        gate_weights = jax.nn.softmax(gate_logits, axis=-1)
        topv, topi = jax.lax.top_k(gate_weights, TOPK)
        h = jax.nn.gelu(jnp.einsum('bsd,ndh->nbsh', x, W1) + b1[:, None, None, :], approximate=False)
        h = jax.nn.gelu(jnp.einsum('nbsh,nhf->nbsf', h, W2) + b2[:, None, None, :], approximate=False)
        eo = jnp.einsum('nbsf,nfd->nbsd', h, W3) + b3[:, None, None, :]
        comb = jnp.sum(jax.nn.one_hot(topi, NE, dtype=x.dtype) * topv[..., None], axis=-2)
        out = jnp.einsum('nbsd,bsn->bsd', eo, comb)
        return out
    x = x + jnp.tanh(g_xattn[0]) * _L0_xattn_ref(_layernorm(x, axis=-1), ctx_2048, ctx_2048)
    x = x + jnp.tanh(g_ffn[0]) * _L0_ffn_ref(_layernorm(x, axis=-1), L0_ffn_base_W, L0_ffn_router_W, L0_ffn_A, L0_ffn_B, L0_ffn_biases)
    x = x + jnp.tanh(g_xattn[1]) * _L1_xattn_ref(ctx_2048, ctx_2048, _layernorm(x, axis=-1), L1_xattn_ssm_kernel, L1_xattn_D, 8)
    x = x + jnp.tanh(g_ffn[1]) * _L1_ffn_ref(_layernorm(x, axis=-1), L1_ffn_W1, L1_ffn_b1, L1_ffn_W2, L1_ffn_b2, L1_ffn_W3, L1_ffn_b3, L1_ffn_Wg, L1_ffn_bg)
    return x

_drawn_inputs = setup_inputs


def setup_inputs(seed=0):
    import zlib

    import numpy as np

    out = dict(_drawn_inputs(seed))
    spreads = {'g_ffn': (-1.0, 0.6),
     'L0_ffn_biases': (0.0, 0.1),
     'L1_ffn_b1': (0.0, 0.8),
     'L1_ffn_b2': (0.0, 2.0),
     'L1_ffn_b3': (0.0, 2.0),
     'L1_ffn_bg': (0.0, 0.8)}
    factors = {'L1_ffn_W1': 8.0, 'L1_ffn_W2': 8.0, 'L1_ffn_W3': 8.0, 'L1_ffn_Wg': 8.0}
    for name, (base, spread) in spreads.items():
        noise = np.random.default_rng([zlib.crc32(name.encode()), seed]).standard_normal(out[name].shape)
        drawn = base * np.exp(spread * noise) if base else spread * noise
        out[name] = jnp.asarray(drawn.astype(out[name].dtype))
    for name, factor in factors.items():
        out[name] = (out[name] * factor).astype(out[name].dtype)
    return out
```

```python
from contextlib import ExitStack

import concourse.bass as bass
from concourse import mybir

F32 = mybir.dt.float32
F32R = mybir.dt.float32r
BF16 = mybir.dt.bfloat16
I32 = mybir.dt.int32
U32 = mybir.dt.uint32
ALU = mybir.AluOpType
ACT = mybir.ActivationFunctionType
AX = mybir.AxisListType

P = 128
EPS = 1e-5
MASKED = -1e30
TAKEN = -3e38


def flamingo_two_layers(nc, x, ctx_2048, ctx_t, ctx_t_rev, g_xattn, g_ffn, lora_w, lora_bt, lora_biases,
                        ssm_kernel, ssm_d, w1, w2, w3, b1, b2, b3, wg, bg, head_halves, out):
    NB, S, DM = x.shape
    assert S == P and DM == 2 * P
    NH, HD = 16, DM // 16
    G = 4
    NG = NH // G
    NR = lora_biases.shape[0]
    NRT = NR // 2
    TOP = 8
    CH = ssm_d.shape[0]
    CD = P // CH
    L = DM
    NE, _, HF = w1.shape
    KF = HF // P
    NT = (2 * NB * S - NE) // P + NE
    SCALING = 2
    OH = HD + 1

    sorted_x = nc.dram_tensor("sorted_x", [NT * P, DM], F32, kind="Internal").ap()
    sorted_y = nc.dram_tensor("sorted_y", [NT * P, DM], F32, kind="Internal").ap()
    kernels = nc.dram_tensor("kernels", [CH, P - 1 + L], F32, kind="Internal").ap()

    with ExitStack() as ctx:
        def sb(name, shape, dt=F32):
            return ctx.enter_context(nc.sbuf_tensor(name, shape, dt))

        def sem(name):
            return ctx.enter_context(nc.semaphore(name))

        X = sb("X", [P, NB, DM])
        HN = sb("HN", [P, NB, DM])
        B1 = sb("B1", [P, NE * HF])
        B2 = sb("B2", [P, NE * HF])
        B3 = sb("B3", [P, NE * DM])
        raw1 = sb("raw1", [P, 2, HF])
        raw2 = sb("raw2", [P, KF, HF])
        raw3 = sb("raw3", [P, KF, DM])
        ident = sb("ident", [P, P])
        identb = sb("identb", [P, P], BF16)
        anti = sb("anti", [P, P])
        causal = sb("causal", [P, G, P], BF16)
        before = sb("before", [P, P], BF16)
        ones = sb("ones", [P, P], BF16)
        halves = sb("halves", [P, 2])
        gates = sb("gates", [P, 4])
        tg = sb("tg", [P, 4])
        lbias = sb("lbias", [P, NR])
        bgb = sb("bgb", [P, NE])
        wg_sb = sb("wg_sb", [P, 2, NE])
        stats = sb("stats", [P, NB, 6])
        mv = sb("mv", [P, NB, 2])
        ve = sb("ve", [P, NB])
        rstd = sb("rstd", [P, NB])
        minus_half = sb("minus_half", [P, NB])
        zeros = sb("zeros", [P, 2048])
        gl = sb("gl", [P, NB, NE])
        gmax = sb("gmax", [P, NB])
        gsum = sb("gsum", [P, NB])
        grec = sb("grec", [P, NB])
        top8 = sb("top8", [P, NB, 8])
        tidx = sb("tidx", [P, NB, 8], U32)
        tidf = sb("tidf", [P, NB, 8])
        wtok = sb("wtok", [P, NB, 2])
        pace = sb("pace", [P, 1])
        iota8 = sb("iota8", [P, NE], I32)
        iota8f = sb("iota8f", [P, NE])
        iota_rows = sb("iota_rows", [P, NE], I32)
        iota_rowsf = sb("iota_rowsf", [P, NE])
        iotat = sb("iotat", [P, 32], I32)
        iotatf = sb("iotatf", [P, 32])
        hot = sb("hot", [P, 2, NB, NE])
        chosen = sb("chosen", [P, NB, NE], BF16)
        over = sb("over", [P, NE, NE])
        tiles_of = sb("tiles_of", [P, NE])
        tiles_to = sb("tiles_to", [P, NE])
        onesr = sb("onesr", [P, NE])
        first_slot = sb("first_slot", [P, NE])
        rank = sb("rank", [P, NB, NE])
        slotf = sb("slotf", [P, NB, NE])
        pick = sb("pick", [P, 2, NB, NE])
        slot2f = sb("slot2f", [P, 2, NB])
        slot2 = sb("slot2", [P, 2, NB], I32)
        past = sb("past", [P, NT, NE])
        etf = sb("etf", [P, NT])
        et = sb("et", [P, NT], I32)
        tiles_to_i = sb("tiles_to_i", [P, NE], I32)

        early = ExitStack()

        def se(name, shape, dt=F32):
            return early.enter_context(nc.sbuf_tensor(name, shape, dt))

        C = se("C", [P, NB, DM])
        ct = [se(f"ct{p}", [P, 2, P]) for p in range(2)]
        va = [se(f"va{p}", [P, NH, OH]) for p in range(2)]
        xn = [se(f"xn{p}", [P, DM]) for p in range(2)]
        qh = [[se(f"qh{p}{o}", [P, 2, P]) for o in range(2)] for p in range(2)]
        pr = [se(f"pr{p}", [P, G, P]) for p in range(2)]
        pt = [se(f"pt{p}", [P, G, P]) for p in range(2)]
        rsum = se("rsum", [P, NB, NH])
        mx = se("mx", [P, 2, G])
        on = se("on", [P, 2, DM])
        HT = se("HT", [P, NB, 2, P])
        LW = se("LW", [P, 2, NRT + NR + DM])
        LB = se("LB", [NR, DM])
        sc = se("sc", [P, NB, NR])
        sg = se("sg", [P, NB, NRT])
        rep = se("rep", [P, NB, NR])
        m8 = se("m8", [P, NB, TOP])
        s8 = se("s8", [P, NB])
        r8 = se("r8", [P, NB])
        mg = se("mg", [P, NB, NR])
        mgT = se("mgT", [NR, NB, P])
        kp = se("kp", [CH, P - 1 + L])
        dcol = se("dcol", [CH, 1])
        CT = se("CT", [P, 2, NB, P])
        QT = se("QT", [P, 2, NB, P])
        us = [se(f"us{p}", [P, L]) for p in range(2)]
        kv = [se(f"kv{p}", [P, 2, NB, CD * CD]) for p in range(2)]
        z = [se(f"z{p}", [P, NB, CD * CD]) for p in range(2)]
        YO = se("YO", [P, 2, NB, P])
        early.close()

        s1h = sb("s1h", [P, 2, 2, HF], F32R)
        s1l = sb("s1l", [P, 2, 2, HF], F32R)
        s2h = sb("s2h", [P, 2, KF, HF], F32R)
        s2l = sb("s2l", [P, 2, KF, HF], F32R)
        s3h = sb("s3h", [P, 2, KF, DM], F32R)
        s3l = sb("s3l", [P, 2, KF, DM], F32R)
        xg = [sb(f"xg{p}", [P, DM]) for p in range(2)]
        xh = [sb(f"xh{p}", [P, 2, P], F32R) for p in range(2)]
        xl = [sb(f"xl{p}", [P, 2, P], F32R) for p in range(2)]
        a1 = [sb(f"a1{p}", [P, HF]) for p in range(2)]
        a2 = [sb(f"a2{p}", [P, HF]) for p in range(2)]
        h1h = sb("h1h", [P, KF, P], F32R)
        h1l = sb("h1l", [P, KF, P], F32R)
        h2h = sb("h2h", [P, KF, P], F32R)
        h2l = sb("h2l", [P, KF, P], F32R)
        yt = [sb(f"yt{p}", [P, DM]) for p in range(2)]
        gy = [sb(f"gy{p}", [P, 2, DM]) for p in range(2)]

        bank = [ctx.enter_context(nc.psum_tensor(f"bank{i}", [P, 512], F32)) for i in range(8)]

        loaded_x = sem("loaded_x")
        loaded_c = sem("loaded_c")
        loaded_ct = [sem("loaded_ct0"), sem("loaded_ct1")]
        loaded_small = sem("loaded_small")
        loaded_lora = sem("loaded_lora")
        loaded_ctx_rev = sem("loaded_ctx_rev")
        loaded_bias = sem("loaded_bias")
        loaded_u = [sem("loaded_u0"), sem("loaded_u1")]
        loaded_w = [sem("loaded_w1"), sem("loaded_w2"), sem("loaded_w3")]
        cleared = sem("cleared")
        consts = sem("consts")
        pool_step = sem("pool_step")
        dve_step = sem("dve_step")
        tanh_done = sem("tanh_done")
        var_done = sem("var_done")
        rstd_done = sem("rstd_done")
        xn_done = sem("xn_done")
        q_turned = sem("q_turned")
        qh_done = sem("qh_done")
        va_done = sem("va_done")
        scores_done = sem("scores_done")
        shifted = sem("shifted")
        probs_done = sem("probs_done")
        p_turned = sem("p_turned")
        pt_done = sem("pt_done")
        pv_done = sem("pv_done")
        attn_done = sem("attn_done")
        normed = sem("normed")
        h_turned = sem("h_turned")
        ht_done = sem("ht_done")
        routed = sem("routed")
        sig_done = sem("sig_done")
        gated = sem("gated")
        g_turned = sem("g_turned")
        mgt_done = sem("mgt_done")
        ffn_done = sem("ffn_done")
        x2_done = sem("x2_done")
        kv_done = sem("kv_done")
        conv_done = sem("conv_done")
        z_done = sem("z_done")
        yo_done = sem("yo_done")
        y_turned = sem("y_turned")
        x3_done = sem("x3_done")
        logits_done = sem("logits_done")
        gexp_done = sem("gexp_done")
        gshift_done = sem("gshift_done")
        chosen_done = sem("chosen_done")
        counted = sem("counted")
        slots_done = sem("slots_done")
        plan_done = sem("plan_done")
        scattered = sem("scattered")
        loaded_xg = [sem("loaded_xg0"), sem("loaded_xg1")]
        x_turned = sem("x_turned")
        xh_done = sem("xh_done")
        xl_done = sem("xl_done")
        l1_done = sem("l1_done")
        l2_done = sem("l2_done")
        l3_done = sem("l3_done")
        a1_done = sem("a1_done")
        a2_done = sem("a2_done")
        g1_done = sem("g1_done")
        g2_done = sem("g2_done")
        h1_turned = sem("h1_turned")
        h2_turned = sem("h2_turned")
        h1h_done = sem("h1h_done")
        h1l_done = sem("h1l_done")
        h2h_done = sem("h2h_done")
        h2l_done = sem("h2l_done")
        y_done = sem("y_done")
        stored_y = [sem("stored_y0"), sem("stored_y1")]
        kernel_row = sem("kernel_row")
        kernels_stored = sem("kernels_stored")
        split_w = [sem("split_w1"), sem("split_w2"), sem("split_w3")]
        gathered = [sem("gathered0"), sem("gathered1")]
        final_done = sem("final_done")
        stored_out = [sem("stored_out0"), sem("stored_out1")]

        CREDIT = 8
        by_dve = (xn_done, shifted, attn_done, z_done, a1_done, a2_done, xl_done, h1l_done, h2l_done, y_done, final_done)
        by_act = (qh_done, probs_done, pt_done, g1_done, g2_done, xh_done, h1h_done, h2h_done)
        by_pe = (q_turned, scores_done, p_turned, pv_done, conv_done, l1_done, l2_done, l3_done, x_turned,
                 h1_turned, h2_turned)
        by_pool = (va_done, kv_done)
        ringed = {s.name for s in by_dve + by_act + by_pe + by_pool}

        def of(s, n):
            assert s.name in ringed
            return n + CREDIT

        def give_credit(eng, sems):
            for s in sems:
                eng.sem_inc(s, CREDIT)

        FULL = 1
        PAIRS = (NT - 4) // 2

        def run_steps(eng, step):
            for t in range(-4, FULL):
                step(t, t % 2, t // 2)
            with eng.Fori(0, PAIRS) as i:
                for q in range(FULL, FULL + 2):
                    step(i * 2 + q, q % 2, i + q // 2)
            for t in range(FULL + 2 * PAIRS, NT + 1):
                step(t, t % 2, t // 2)

        def exists(t):
            return not isinstance(t, int) or 0 <= t < NT

        block = ctx.enter_context(nc.Block())

        def to_all(ap, n):
            return bass.AP(ap.tensor, ap.offset, [[0, P], [1, n]])

        N_SMALL = 7
        N_CLEAR = -(-NT * DM // 2048)

        @block.sync
        def _(sp):
            sp.dma_start(X[:, :, :], x.rearrange("b p d -> p b d")).then_inc(loaded_x, 16)
            sp.dma_start(halves[:, :], head_halves).then_inc(loaded_small, 16)
            sp.dma_start(gates[:, 0:2], to_all(g_xattn, 2)).then_inc(loaded_small, 16)
            sp.dma_start(gates[:, 2:4], to_all(g_ffn, 2)).then_inc(loaded_small, 16)
            sp.dma_start(C[:, :, :], ctx_2048.rearrange("b p d -> p b d")).then_inc(loaded_c, 16)
            sp.dma_start(lbias[:, :], to_all(lora_biases, NR)).then_inc(loaded_small, 16)
            sp.dma_start(bgb[:, :], to_all(bg, NE)).then_inc(loaded_small, 16)
            sp.dma_start(wg_sb[:, :, :], wg.rearrange("(c p) n -> p c n", p=P)).then_inc(loaded_small, 16)
            sp.dma_start(LB[:, :], lora_bt).then_inc(loaded_small, 16)
            with sp.Fori(0, NB // 2) as i:
                for p in range(2):
                    sp.wait_ge(scores_done, of(scores_done, i * 2 * NG + (p * NG - NG)))
                    src = ctx_t[bass.ds(2 * i + p, 1), :, :].rearrange("o (c p) s -> p (o c) s", p=P)
                    sp.dma_start(ct[p][:, :, :], src).then_inc(loaded_ct[p], 16)
            sp.dma_start(LW[:, :, :], lora_w.rearrange("(c p) n -> p c n", p=P)).then_inc(loaded_lora, 16)
            for b in range(NB):
                sp.dma_start(CT[:, :, b, :], ctx_t_rev[b].rearrange("(c p) s -> p c s", p=P)).then_inc(loaded_ctx_rev, 16)
            sp.wait_ge(consts, 1)
            sp.dma_start(kp[:, P - 1:P - 1 + L], ssm_kernel).then_inc(kernel_row, 16)
            sp.dma_start(dcol[:, :], ssm_d.rearrange("(h o) -> h o", o=1)).then_inc(kernel_row, 16)
            rows = sorted_x.rearrange("(t p) d -> p t d", p=P)
            for t in range(0, NT, 2048 // DM):
                n = min(2048 // DM, NT - t)
                sp.dma_start(rows[:, t:t + n, :], zeros[:, 0:n * DM].rearrange("p (t d) -> p t d", d=DM)).then_inc(cleared, 16)
            sp.dma_start(B1[:, :], to_all(b1, NE * HF)).then_inc(loaded_bias, 16)
            sp.dma_start(B2[:, :], to_all(b2, NE * HF)).then_inc(loaded_bias, 16)
            sp.dma_start(B3[:, :], to_all(b3, NE * DM)).then_inc(loaded_bias, 16)
            sp.wait_ge(kernel_row, 33)
            sp.dma_start(kernels, kp[:, :]).then_inc(kernels_stored, 16)
            sp.wait_ge(kernels_stored, 16)
            with sp.Fori(0, CH // 2) as i:
                for p in range(2):
                    sp.wait_ge(conv_done, of(conv_done, i * 4 + (2 * p - 2)))
                    src = bass.AP(kernels.tensor, (2 * i + p) * (P - 1 + L), [[1, P], [1, L]])
                    sp.dma_start(us[p][:, :], src).then_inc(loaded_u[p], 16)
            sp.wait_ge(scattered, 16 * 2 * NB)

            def step(t, par, half):
                if exists(t + 4):
                    sp.wait_ge(x_turned, of(x_turned, t + 3))
                    sp.dma_start(xg[par][:, :], sorted_x[bass.ts(t + 4, P), :]).then_inc(loaded_xg[par], 16)
                if exists(t - 1):
                    sp.wait_ge(y_done, of(y_done, t))
                    sp.dma_start(sorted_y[bass.ts(t - 1, P), :], yt[1 - par][:, :]).then_inc(stored_y[1 - par], 16)

            run_steps(sp, step)
            for b in range(NB):
                sp.wait_ge(final_done, of(final_done, b + 1))
                sp.dma_start(out[b], X[:, b, :]).then_inc(stored_out[b % 2], 16)
            for p in range(2):
                sp.wait_ge(stored_out[p], 16 * NB // 2)

        @block.gpsimd
        def _(pool):
            give_credit(pool, by_pool)
            n_after = [0]

            def after(ins):
                n_after[0] += 1
                ins.then_inc(pool_step, 1)
                pool.wait_ge(pool_step, n_after[0])

            pool.memset(kp[:, :], 0.0)
            pool.memset(zeros[:, :], 0.0).then_inc(consts, 1)
            pool.memset(minus_half[:, :], -0.5)
            pool.memset(onesr[:, :], 1.0)
            pool.memset(ident[:, :], 0.0)
            pool.memset(identb[:, :], 0.0)
            pool.memset(causal[:, :, :], 0.0)
            pool.memset(ones[:, :], 1.0)
            for p in range(2):
                pool.memset(va[p][:, :, HD:OH], 1.0)
            after(pool.memset(before[:, :], 1.0))
            pool.affine_select(out=ident[:, :], in_=ident[:, :], compare_op=ALU.not_equal, fill=1.0, base=0,
                               pattern=[[-1, P]], channel_multiplier=1)
            pool.affine_select(out=identb[:, :], in_=identb[:, :], compare_op=ALU.not_equal, fill=1.0, base=0,
                               pattern=[[-1, P]], channel_multiplier=1)
            pool.affine_select(out=causal[:, :, :], in_=causal[:, :, :], compare_op=ALU.is_ge, fill=MASKED, base=0,
                               pattern=[[0, G], [-1, P]], channel_multiplier=1)
            pool.affine_select(out=before[:, :], in_=before[:, :], compare_op=ALU.is_gt, fill=0.0, base=0,
                               pattern=[[1, P]], channel_multiplier=-1)
            pool.iota(iota8[:, :], pattern=[[1, NE]], base=0, channel_multiplier=0)
            pool.iota(iota_rows[:, :], pattern=[[P, NE]], base=0, channel_multiplier=0)
            pool.iota(iotat[:, :], pattern=[[1, 32]], base=0, channel_multiplier=0).then_inc(consts, 1)

            for raw, w, loaded in ((raw1, w1, loaded_w[0]), (raw2, w2, loaded_w[1]), (raw3, w3, loaded_w[2])):
                pool.dma_start(raw[:, :, :], w[0].rearrange("(c p) n -> p c n", p=P)).then_inc(loaded, 16)

            norms = [0]

            def inverse_deviation():
                norms[0] += 1
                pool.wait_ge(var_done, norms[0])
                pool.tensor_tensor(rstd[:, :], ve[:, :], minus_half[:, :], ALU.pow).then_inc(rstd_done, 1)

            inverse_deviation()
            with pool.Fori(0, NB // 2) as i:
                for p in range(2):
                    pool.wait_ge(pv_done, of(pv_done, i * 2 * NG + (p * NG - NG)))
                    pool.wait_ge(loaded_c, 16)
                    src = C[:, bass.ds(2 * i + p, 1), :].rearrange("p o (h d) -> p (o h) d", d=HD)
                    pool.tensor_copy(va[p][:, :, 0:HD], src).then_inc(va_done, 1)
            inverse_deviation()
            inverse_deviation()
            pool.wait_ge(loaded_ctx_rev, 16 * NB)
            with pool.Fori(0, CH // 2) as i:
                for p in range(2):
                    pool.wait_ge(conv_done, of(conv_done, i * 4 + (2 * p - 2)))
                    for c in range(2):
                        kk = CT[:, c, :, bass.ds((2 * i + p) * CD, CD)]
                        o = kv[p][:, c, :, :].rearrange("p b (i j) -> p b i j", j=CD)
                        shape = [P, NB, CD, CD]
                        pool.tensor_tensor(o, kk.unsqueeze(3).broadcast_to(shape), kk.unsqueeze(2).broadcast_to(shape),
                                           ALU.mult).then_inc(kv_done, 1)
            inverse_deviation()

            pool.wait_ge(cleared, 16 * N_CLEAR)
            pool.wait_ge(slots_done, 1)
            for b in range(NB):
                for k in range(2):
                    pool.indirect_dma_start(out=sorted_x, out_offset=bass.IndirectOffsetOnAxis(ap=slot2[:, k, b:b + 1], axis=0),
                                            in_=HN[:, b, :], in_offset=None).then_inc(scattered, 16)

            parts = ((raw1, s1h, s1l, loaded_w[0], split_w[0]), (raw2, s2h, s2l, loaded_w[1], split_w[1]),
                     (raw3, s3h, s3l, loaded_w[2], split_w[2]))

            def split(e, k):
                raw, high, low, loaded, done = parts[k]
                pool.wait_ge(loaded, (e + 1) * 16)
                pool.tensor_copy(high[:, e % 2, :, :], raw[:, :, :]).then_inc(done, 1)
                pool.wait_ge(done, 2 * e + 1)
                pool.tensor_tensor(low[:, e % 2, :, :], raw[:, :, :], high[:, e % 2, :, :].bitcast(F32),
                                   ALU.subtract).then_inc(done, 1)
                if e + 1 < NE:
                    pool.wait_ge(done, 2 * e + 2)
                    pool.dma_start(raw[:, :, :], (w1, w2, w3)[k][e + 1].rearrange("(c p) n -> p c n", p=P)).then_inc(loaded, 16)

            for e in range(2):
                for k in range(3):
                    split(e, k)
            pool.wait_ge(plan_done, 1)
            for e in range(2, NE):
                last = pool.value_load(tiles_to_i[0:1, e - 2:e - 1], min_val=1, max_val=NT)
                for k, passed in enumerate((l1_done, l2_done, l3_done)):
                    pool.wait_ge(passed, of(passed, last))
                    pool.tensor_tensor(pace[:, :], onesr[:, 0:1], onesr[:, 0:1], ALU.mult)
                    split(e, k)
            for p in range(2):
                pool.wait_ge(stored_y[p], 16 * ((NT + 1 - p) // 2))
            for b in range(NB):
                pool.wait_ge(final_done, of(final_done, b - 1))
                for k in range(2):
                    pool.indirect_dma_start(out=gy[b % 2][:, k, :], out_offset=None, in_=sorted_y,
                                            in_offset=bass.IndirectOffsetOnAxis(ap=slot2[:, k, b:b + 1], axis=0)
                                            ).then_inc(gathered[b % 2], 16)

        @block.tensor
        def _(pe):
            give_credit(pe, by_pe)
            TQ, SB, PTB, OB = bank[0:2], bank[2:4], bank[4:6], bank[6:8]
            pe.wait_ge(consts, 2)
            with pe.Fori(0, NB // 2) as i:
                def turn_q(p):
                    pe.wait_ge(xn_done, of(xn_done, i * 2 + (p + 1)))
                    pe.wait_ge(qh_done, of(qh_done, i * 4 + (2 * p - 2)))
                    for c in range(2):
                        last = pe.transpose(TQ[p][:, c * P:(c + 1) * P], xn[p][:, c * P:(c + 1) * P], ident[:, :])
                    last.then_inc(q_turned, 1)

                def scores(n):
                    p, r = n // NG, n % NG
                    if r == 0:
                        pe.wait_ge(loaded_ct[p], i * 16 + 16)
                        pe.wait_ge(qh_done, of(qh_done, i * 4 + (2 * p + 2)))
                    pe.wait_ge(shifted, of(shifted, i * 2 * NG + (n - 1)))
                    o = SB[n % 2]
                    pe.matmul(o[:, :], identb[:, :], causal[:, :, :].rearrange("p g k -> p (g k)"), start=True, stop=False,
                              skip_group_check=True)
                    for j in range(G):
                        c, odd = j // 2, j % 2
                        last = pe.matmul(o[:, j * P:(j + 1) * P], qh[p][odd][32 * r:32 * r + 32, c, :],
                                         ct[p][32 * r:32 * r + 32, c, :], start=False, stop=(j == G - 1), skip_group_check=True)
                    last.then_inc(scores_done, 1)

                def turn_p(n):
                    pe.wait_ge(probs_done, of(probs_done, i * 2 * NG + (n + 1)))
                    pe.wait_ge(pt_done, of(pt_done, i * 2 * NG + (n - 1)))
                    for j in range(G):
                        last = pe.transpose(PTB[n % 2][:, j * P:(j + 1) * P], pr[n % 2][:, j, :], ident[:, :])
                    last.then_inc(p_turned, 1)

                def values(n):
                    p, r = n // NG, n % NG
                    if r == 0:
                        pe.wait_ge(va_done, of(va_done, i * 2 + (p + 1)))
                        pe.wait_ge(attn_done, of(attn_done, i * 2 + (p - 1)))
                    pe.wait_ge(pt_done, of(pt_done, i * 2 * NG + (n + 1)))
                    for j in range(G):
                        h = 8 * (j // 2) + 2 * r + j % 2
                        last = pe.matmul(OB[p][:, h * OH:(h + 1) * OH], pt[n % 2][:, j, :], va[p][:, h, :],
                                         start=True, stop=True, skip_group_check=True)
                    last.then_inc(pv_done, 1)

                turn_q(0)
                turn_q(1)
                for n in range(2 * NG + 3):
                    if n < 2 * NG:
                        scores(n)
                    if 2 <= n < 2 * NG + 2:
                        turn_p(n - 2)
                    if n >= 3:
                        values(n - 3)

            pairs = [0]

            def turn_norm(banks):
                first = 2 * pairs[0]
                for b in range(NB):
                    pe.wait_ge(normed, first + b + 1)
                    if b >= 4 and b % 2 == 0:
                        pe.wait_ge(ht_done, pairs[0] - 1)
                    for c in range(2):
                        last = pe.transpose(banks[(b // 2) % 2][:, (2 * (b % 2) + c) * P:(2 * (b % 2) + c + 1) * P],
                                            HN[:, b, c * P:(c + 1) * P], ident[:, :])
                    if b % 2:
                        pairs[0] += 1
                        last.then_inc(h_turned, 1)

            turn_norm(bank[0:2])
            pe.wait_ge(loaded_lora, 16)
            pe.wait_ge(loaded_small, 16 * N_SMALL)
            pe.wait_ge(attn_done, of(attn_done, NB))
            NW = NRT + NR
            for b in range(NB):
                if b % 2 == 0:
                    pe.wait_ge(ht_done, b // 2 + 1)
                for c in range(2):
                    last = pe.matmul(bank[2 + b // 4][:, (b % 4) * P:(b % 4) * P + NW], HT[:, b, c, :], LW[:, c, 0:NW],
                                     start=(c == 0), stop=(c == 1), skip_group_check=True)
                if b % 4 == 3:
                    last.then_inc(routed, 1)
            for b in range(NB):
                pe.wait_ge(gated, b + 1)
                last = pe.transpose(bank[b // 4][0:NR, (b % 4) * P:(b % 4 + 1) * P], mg[:, b, :], ident[:, :])
                if b % 4 == 3:
                    last.then_inc(g_turned, 1)
            for b in range(NB):
                o = bank[4 + b // 2][:, (b % 2) * DM:(b % 2 + 1) * DM]
                for c in range(2):
                    pe.matmul(o, HT[:, b, c, :], LW[:, c, NW:NW + DM], start=(c == 0), stop=False, skip_group_check=True)
                if b % 4 == 0:
                    pe.wait_ge(mgt_done, b // 4 + 1)
                last = pe.matmul(o, mgT[:, b, :], LB[:, :], start=False, stop=True, skip_group_check=True)
                if b % 2:
                    last.then_inc(ffn_done, 1)

            turn_norm(bank[0:2])
            pe.wait_ge(x2_done, 1)
            YB = bank[2:6]
            with pe.Fori(0, CH // 2) as i:
                for p in range(2):
                    pe.wait_ge(loaded_u[p], i * 16 + 16)
                    for c in range(2):
                        n = 2 * p + c
                        pe.wait_ge(kv_done, of(kv_done, i * 4 + (n + 1)))
                        pe.wait_ge(z_done, of(z_done, i * 4 + (n - 3)))
                        o = YB[n][:, :]
                        rhs = kv[p][:, :, :, :].rearrange("p c b k -> p c (b k)")
                        if c == 0:
                            last = pe.matmul(o, us[p][:, 0:P], rhs[:, 0, :], start=True, stop=True)
                        else:
                            pe.matmul(o, us[p][:, P:2 * P], rhs[:, 0, :], start=True, stop=False)
                            last = pe.matmul(o, us[p][:, 0:P], rhs[:, 1, :], start=False, stop=True)
                        last.then_inc(conv_done, 1)
            pe.wait_ge(yo_done, 1)
            for b in range(NB):
                if b >= 4:
                    pe.wait_ge(x3_done, b - 3)
                for c in range(2):
                    last = pe.transpose(bank[b % 4][:, c * P:(c + 1) * P], YO[:, c, b, :], ident[:, :])
                last.then_inc(y_turned, 1)

            turn_norm(bank[4:6])
            for b in range(NB):
                if b % 2 == 0:
                    pe.wait_ge(ht_done, 8 + b // 2 + 1)
                for c in range(2):
                    last = pe.matmul(bank[6][:, b * NE:(b + 1) * NE], HT[:, b, c, :], wg_sb[:, c, :],
                                     start=(c == 0), stop=(c == 1), skip_group_check=True)
            last.then_inc(logits_done, 1)
            pe.wait_ge(chosen_done, 1)
            pe.matmul(bank[7][:, 0:NB * NE], before[:, :], chosen[:, :, :].rearrange("p b e -> p (b e)"), start=True,
                      stop=False, skip_group_check=True)
            for b in range(NB - 1):
                for b2 in range(b + 1, NB):
                    pe.matmul(bank[7][:, b2 * NE:(b2 + 1) * NE], ones[:, :], chosen[:, b, :],
                              start=False, stop=(b == NB - 2), skip_group_check=True)
            for b in range(NB):
                last = pe.matmul(bank[4][:, 0:NE], ones[:, :], chosen[:, b, :], start=(b == 0), stop=(b == NB - 1))
            last.then_inc(counted, 1)

            pe.wait_ge(plan_done, 1)

            def expert(t):
                return pe.value_load(et[0:1, bass.ds(t, 1)], min_val=0, max_val=NE - 1)

            def layer(e, k, o, high, low, w_high, w_low, n_k, done):
                pe.wait_ge(split_w[k], e * 2 + 2)
                for j in range(n_k):
                    for m, (a, w) in enumerate(((high, w_high), (high, w_low), (low, w_high))):
                        last = pe.matmul(o, a[:, j, :], w[:, bass.ds(e % 2, 1), j, :].rearrange("p o n -> p (o n)"),
                                         start=(j == 0 and m == 0), stop=(j == n_k - 1 and m == 2))
                last.then_inc(done, 1)

            def turn(o, src, n_k, done):
                for j in range(n_k):
                    last = pe.transpose(o[:, j * P:(j + 1) * P], src[:, j * P:(j + 1) * P], ident[:, :])
                last.then_inc(done, 1)

            def step(t, par, half):
                if exists(t):
                    e = expert(t)
                    pe.wait_ge(h1h_done, of(h1h_done, t + 1))
                    pe.wait_ge(h1l_done, of(h1l_done, t + 1))
                    pe.wait_ge(a2_done, of(a2_done, t))
                    layer(e, 1, bank[4][:, :], h1h, h1l, s2h, s2l, KF, l2_done)
                if exists(t - 1):
                    e = expert(t - 1)
                    pe.wait_ge(h2h_done, of(h2h_done, t))
                    pe.wait_ge(h2l_done, of(h2l_done, t))
                    pe.wait_ge(y_done, of(y_done, t - 1))
                    layer(e, 2, bank[5][:, 0:DM], h2h, h2l, s3h, s3l, KF, l3_done)
                if exists(t + 1):
                    pe.wait_ge(g1_done, of(g1_done, t + 2))
                    pe.wait_ge(h1l_done, of(h1l_done, t + 1))
                    turn(bank[1], a1[1 - par], KF, h1_turned)
                if exists(t):
                    pe.wait_ge(g2_done, of(g2_done, t + 1))
                    pe.wait_ge(h2l_done, of(h2l_done, t))
                    turn(bank[2], a2[par], KF, h2_turned)
                if exists(t + 3):
                    pe.wait_ge(loaded_xg[1 - par], 16 * (half + (par + 3) // 2 + 1))
                    pe.wait_ge(xl_done, of(xl_done, t + 3))
                    turn(bank[0], xg[1 - par], 2, x_turned)
                if exists(t + 2):
                    e = expert(t + 2)
                    pe.wait_ge(xh_done, of(xh_done, t + 3))
                    pe.wait_ge(xl_done, of(xl_done, t + 3))
                    pe.wait_ge(a1_done, of(a1_done, t + 2))
                    layer(e, 0, bank[3][:, :], xh[par], xl[par], s1h, s1l, 2, l1_done)

            run_steps(pe, step)

        @block.scalar
        def _(act):
            give_credit(act, by_act)
            act.wait_ge(loaded_small, 16 * N_SMALL)
            act.activation(tg[:, :], gates[:, :], ACT.Tanh).then_inc(tanh_done, 1)
            with act.Fori(0, NB // 2) as i:
                def queries(p):
                    act.wait_ge(q_turned, of(q_turned, i * 2 + (p + 1)))
                    act.wait_ge(scores_done, of(scores_done, i * 2 * NG + (p * NG - NG)))
                    for odd in range(2):
                        act.activation(qh[p][odd][:, :, :], bank[p][:, 0:DM].rearrange("p (c s) -> p c s", c=2), ACT.Copy,
                                       scale=halves[:, odd:odd + 1]).then_inc(qh_done, 1)

                def probs(n):
                    act.wait_ge(shifted, of(shifted, i * 2 * NG + (n + 1)))
                    act.activation(pr[n % 2][:, :, :], pr[n % 2][:, :, :], ACT.Exp).then_inc(probs_done, 1)

                def probs_turned(n):
                    act.wait_ge(p_turned, of(p_turned, i * 2 * NG + (n + 1)))
                    act.wait_ge(pv_done, of(pv_done, i * 2 * NG + (n - 1)))
                    act.activation(pt[n % 2][:, :, :], bank[4 + n % 2][:, :].rearrange("p (g s) -> p g s", g=G),
                                   ACT.Copy).then_inc(pt_done, 1)

                queries(0)
                queries(1)
                for n in range(2 * NG + 2):
                    if n < 2 * NG:
                        probs(n)
                    if n >= 2:
                        probs_turned(n - 2)

            copied = [0]

            def copy_turned(banks, dst):
                for k in range(NB // 2):
                    copied[0] += 1
                    act.wait_ge(h_turned, copied[0])
                    act.activation(dst(k), banks[k % 2][:, :].rearrange("p (b c s) -> p b c s", b=2, c=2),
                                   ACT.Copy).then_inc(ht_done, 1)

            copy_turned(bank[0:2], lambda k: HT[:, 2 * k:2 * k + 2, :, :])
            for k in range(2):
                act.wait_ge(routed, k + 1)
                act.activation(sg[:, 4 * k:4 * k + 4, :], bank[2 + k][:, :].rearrange("p (b n) -> p b n", b=4)[:, :, 0:NRT],
                               ACT.Exp, scale=-1.0).then_inc(sig_done, 1)
            for k in range(2):
                act.wait_ge(g_turned, k + 1)
                act.activation(mgT[:, 4 * k:4 * k + 4, :], bank[k][0:NR, :].rearrange("p (b s) -> p b s", b=4),
                               ACT.Copy).then_inc(mgt_done, 1)
            copy_turned(bank[0:2], lambda k: QT[:, :, 2 * k:2 * k + 2, :].rearrange("p c b s -> p b c s"))
            copy_turned(bank[4:6], lambda k: HT[:, 2 * k:2 * k + 2, :, :])
            act.wait_ge(gshift_done, 1)
            act.activation(gl[:, :, :], gl[:, :, :], ACT.Exp).then_inc(gexp_done, 1)

            def step(t, par, half):
                if exists(t):
                    act.wait_ge(a2_done, of(a2_done, t + 1))
                    act.activation(a2[par][:, :], a2[par][:, :], ACT.Gelu).then_inc(g2_done, 1)
                if exists(t + 1):
                    act.wait_ge(h1_turned, of(h1_turned, t + 2))
                    act.wait_ge(l2_done, of(l2_done, t + 1))
                    act.activation(h1h[:, :, :], bank[1][:, :].rearrange("p (k s) -> p k s", k=KF), ACT.Copy).then_inc(h1h_done, 1)
                if exists(t):
                    act.wait_ge(h2_turned, of(h2_turned, t + 1))
                    act.wait_ge(l3_done, of(l3_done, t))
                    act.activation(h2h[:, :, :], bank[2][:, :].rearrange("p (k s) -> p k s", k=KF), ACT.Copy).then_inc(h2h_done, 1)
                if exists(t + 3):
                    act.wait_ge(x_turned, of(x_turned, t + 4))
                    act.wait_ge(l1_done, of(l1_done, t + 2))
                    act.activation(xh[1 - par][:, :, :], bank[0][:, 0:DM].rearrange("p (c s) -> p c s", c=2),
                                   ACT.Copy).then_inc(xh_done, 1)
                if exists(t + 2):
                    act.wait_ge(a1_done, of(a1_done, t + 3))
                    act.activation(a1[par][:, :], a1[par][:, :], ACT.Gelu).then_inc(g1_done, 1)

            run_steps(act, step)

        @block.vector
        def _(dve):
            give_credit(dve, by_dve)
            n_after = [0]

            def after(ins):
                n_after[0] += 1
                ins.then_inc(dve_step, 1)
                dve.wait_ge(dve_step, n_after[0])

            norms = [0]

            def deviations():
                for b in range(NB):
                    ins = dve.bn_stats(stats[:, b, :], X[:, b, :])
                after(ins)
                for b in range(NB):
                    ins = dve.bn_aggr(mv[:, b, :], stats[:, b, :])
                after(ins)
                dve.tensor_scalar(ve[:, :], mv[:, :, 1], EPS, None, ALU.add).then_inc(var_done, 1)
                norms[0] += 1
                dve.wait_ge(rstd_done, norms[0])

            def norm_all():
                deviations()
                for b in range(NB):
                    dve.tensor_scalar(HN[:, b, :], X[:, b, :], mv[:, b, 0:1], rstd[:, b:b + 1], ALU.subtract,
                                      ALU.mult).then_inc(normed, 1)

            dve.wait_ge(loaded_x, 16)
            deviations()
            A_STEPS = 2 * NG + 2 * 3
            first_step = n_after[0]
            with dve.Fori(0, NB // 2) as i:
                k_after = [0]

                def then(ins):
                    k_after[0] += 1
                    ins.then_inc(dve_step, 1)
                    dve.wait_ge(dve_step, i * A_STEPS + (first_step + k_after[0]))

                def normalise(p):
                    dve.wait_ge(q_turned, of(q_turned, i * 2 + (p - 1)))
                    b = 2 * i + p
                    dve.tensor_scalar(xn[p][:, :], X[:, bass.ds(b, 1), :].rearrange("p o d -> p (o d)"),
                                      mv[:, bass.ds(b, 1), 0:1].rearrange("p o d -> p (o d)"), rstd[:, bass.ds(b, 1)],
                                      ALU.subtract, ALU.mult).then_inc(xn_done, 1)

                def shift(n):
                    dve.wait_ge(scores_done, of(scores_done, i * 2 * NG + (n + 1)))
                    s = bank[2 + n % 2][:, :].rearrange("p (g k) -> p g k", g=G)
                    then(dve.tensor_reduce(mx[:, n % 2, :], s, AX.X, ALU.max))
                    dve.wait_ge(p_turned, of(p_turned, i * 2 * NG + (n - 1)))
                    dve.tensor_tensor(pr[n % 2][:, :, :], s, mx[:, n % 2, :].unsqueeze(2).broadcast_to([P, G, P]),
                                      ALU.subtract).then_inc(shifted, 1)

                def add_attention(p):
                    dve.wait_ge(pv_done, of(pv_done, i * 2 * NG + (p + 1) * NG))
                    o = bank[6 + p][:, 0:NH * OH].rearrange("p (h d) -> p h d", d=OH)
                    then(dve.reciprocal(rsum[:, p, :], o[:, :, HD]))
                    then(dve.tensor_scalar(rsum[:, p, :], rsum[:, p, :], tg[:, 0:1], None, ALU.mult))
                    then(dve.tensor_tensor(on[:, p, :].rearrange("p (h d) -> p h d", d=HD), o[:, :, 0:HD],
                                           rsum[:, p, :].unsqueeze(2).broadcast_to([P, NH, HD]), ALU.mult))
                    xb = X[:, bass.ds(2 * i + p, 1), :].rearrange("p o d -> p (o d)")
                    dve.tensor_tensor(xb, on[:, p, :], xb, ALU.add).then_inc(attn_done, 1)

                normalise(0)
                normalise(1)
                for n in range(2 * NG):
                    shift(n)
                    if n == NG + 3:
                        add_attention(0)
                add_attention(1)
                assert k_after[0] == A_STEPS
            n_after[0] = first_step + (NB // 2) * A_STEPS
            dve.wait_ge(attn_done, of(attn_done, NB))

            norm_all()
            dve.wait_ge(sig_done, 2)
            after(dve.tensor_scalar(sg[:, :, :], sg[:, :, :], 1.0, None, ALU.add))
            after(dve.reciprocal(sg[:, :, :], sg[:, :, :]))
            shape = [P, NB, NRT, 2]
            after(dve.tensor_tensor(sc[:, :, :].rearrange("p b (n r) -> p b n r", r=2), sg[:, :, :].unsqueeze(3).broadcast_to(shape),
                                    lbias[:, :].rearrange("p (n r) -> p n r", r=2).unsqueeze(1).broadcast_to(shape), ALU.add))
            for b in range(NB):
                ins = dve.max(m8[:, b, :], sc[:, b, :])
            after(ins)
            dve.tensor_reduce(s8[:, :], m8[:, :, :], AX.X, ALU.add)
            for b in range(NB):
                ins = dve.match_replace(rep[:, b, :], m8[:, b, :], sc[:, b, :], TAKEN)
            after(ins)
            after(dve.reciprocal(r8[:, :], s8[:, :]))
            dve.tensor_scalar(r8[:, :], r8[:, :], float(TOP * SCALING), None, ALU.mult)
            after(dve.scalar_tensor_tensor(out=rep[:, :, :], in0=rep[:, :, :], scalar=TAKEN, in1=sc[:, :, :],
                                           op0=ALU.is_equal, op1=ALU.mult))
            for b in range(NB):
                mid = bank[2 + b // 4][:, (b % 4) * P + NRT:(b % 4) * P + NRT + NR]
                dve.scalar_tensor_tensor(out=mg[:, b, :], in0=rep[:, b, :], scalar=r8[:, b:b + 1], in1=mid,
                                         op0=ALU.mult, op1=ALU.mult).then_inc(gated, 1)
            for b in range(NB):
                if b % 2 == 0:
                    dve.wait_ge(ffn_done, b // 2 + 1)
                ins = dve.scalar_tensor_tensor(out=X[:, b, :], in0=bank[4 + b // 2][:, (b % 2) * DM:(b % 2 + 1) * DM],
                                               scalar=tg[:, 2:3], in1=X[:, b, :], op0=ALU.mult, op1=ALU.add)
            ins.then_inc(x2_done, 1)
            dve.wait_ge(x2_done, 1)

            norm_all()
            dve.wait_ge(kernel_row, 32)
            dve.tensor_tensor(kp[:, P - 1:P], kp[:, P - 1:P], dcol[:, :], ALU.add).then_inc(kernel_row, 1)
            dve.wait_ge(ht_done, 8)
            C_STEPS = 4
            first_step2 = n_after[0]
            with dve.Fori(0, CH // 2) as i:
                for n in range(4):
                    p, c = n // 2, n % 2
                    cols = bass.ds((2 * i + p) * CD, CD)
                    dve.wait_ge(conv_done, of(conv_done, i * 4 + (n + 1)))
                    shape = [P, NB, CD, CD]
                    zz = z[n % 2][:, :, :].rearrange("p b (i j) -> p b i j", j=CD)
                    dve.tensor_tensor(zz, bank[2 + n][:, :].rearrange("p (b i j) -> p b i j", b=NB, j=CD),
                                      QT[:, c, :, cols].unsqueeze(3).broadcast_to(shape), ALU.mult).then_inc(z_done, 1)
                    dve.wait_ge(z_done, of(z_done, i * 4 + (n + 1)))
                    dve.tensor_reduce(YO[:, c, :, cols], zz.rearrange("p b i j -> p b j i"), AX.X, ALU.add).then_inc(dve_step, 1)
            n_after[0] = first_step2 + (CH // 2) * C_STEPS
            dve.wait_ge(dve_step, n_after[0])
            dve.tensor_copy(iota8f[:, :], iota8[:, :]).then_inc(yo_done, 1)
            dve.tensor_copy(iota_rowsf[:, :], iota_rows[:, :])
            after(dve.tensor_copy(iotatf[:, :], iotat[:, :]))
            for b in range(NB):
                dve.wait_ge(y_turned, b + 1)
                ins = dve.scalar_tensor_tensor(out=X[:, b, :], in0=bank[b % 4][:, 0:DM], scalar=tg[:, 1:2], in1=X[:, b, :],
                                               op0=ALU.mult, op1=ALU.add).then_inc(x3_done, 1)
            dve.wait_ge(x3_done, NB)

            norm_all()
            dve.wait_ge(logits_done, 1)
            by_e = [P, NB, NE]
            after(dve.tensor_tensor(gl[:, :, :], bank[6][:, 0:NB * NE].rearrange("p (b e) -> p b e", e=NE),
                                    bgb[:, :].unsqueeze(1).broadcast_to(by_e), ALU.add))
            after(dve.tensor_reduce(gmax[:, :], gl[:, :, :], AX.X, ALU.max))
            dve.tensor_tensor(gl[:, :, :], gl[:, :, :], gmax[:, :].unsqueeze(2).broadcast_to(by_e), ALU.subtract).then_inc(gshift_done, 1)
            dve.wait_ge(gexp_done, 1)
            after(dve.tensor_reduce(gsum[:, :], gl[:, :, :], AX.X, ALU.add))
            after(dve.reciprocal(grec[:, :], gsum[:, :]))
            after(dve.tensor_tensor(gl[:, :, :], gl[:, :, :], grec[:, :].unsqueeze(2).broadcast_to(by_e), ALU.mult))
            for b in range(NB):
                ins = dve.max(top8[:, b, :], gl[:, b, :])
            after(ins)
            dve.tensor_scalar(wtok[:, :, :], top8[:, :, 0:2], tg[:, 3:4], None, ALU.mult)
            for b in range(NB):
                ins = dve.max_index(tidx[:, b, :], top8[:, b, :], gl[:, b, :])
            after(ins)
            after(dve.tensor_copy(tidf[:, :, :], tidx[:, :, :]))
            for k in range(2):
                ins = dve.tensor_tensor(hot[:, k, :, :], iota8f[:, :].unsqueeze(1).broadcast_to(by_e),
                                        tidf[:, :, k].unsqueeze(2).broadcast_to(by_e), ALU.is_equal)
            after(ins)
            dve.tensor_tensor(chosen[:, :, :], hot[:, 0, :, :], hot[:, 1, :, :], ALU.add).then_inc(chosen_done, 1)
            dve.wait_ge(counted, 1)
            e_by_j = [P, NE, NE]
            after(dve.tensor_tensor(over[:, :, :], bank[4][:, 0:NE].unsqueeze(2).broadcast_to(e_by_j),
                                    iota_rowsf[:, :].unsqueeze(1).broadcast_to(e_by_j), ALU.is_gt))
            after(dve.tensor_reduce(tiles_of[:, :], over[:, :, :], AX.X, ALU.add))
            after(dve.tensor_scalar(tiles_of[:, :], tiles_of[:, :], 1.0, None, ALU.max))
            after(dve.tensor_tensor_scan(tiles_to[:, :], onesr[:, :], tiles_of[:, :], 0.0, ALU.mult, ALU.add))
            after(dve.tensor_tensor(first_slot[:, :], tiles_to[:, :], tiles_of[:, :], ALU.subtract))
            after(dve.tensor_scalar(first_slot[:, :], first_slot[:, :], float(P), None, ALU.mult))
            after(dve.tensor_tensor(slotf[:, :, :], bank[7][:, 0:NB * NE].rearrange("p (b e) -> p b e", e=NE),
                                    first_slot[:, :].unsqueeze(1).broadcast_to(by_e), ALU.add))
            for k in range(2):
                ins = dve.tensor_tensor(pick[:, k, :, :], hot[:, k, :, :], slotf[:, :, :], ALU.mult)
            after(ins)
            after(dve.tensor_reduce(slot2f[:, :, :], pick[:, :, :, :], AX.X, ALU.add))
            dve.tensor_copy(slot2[:, :, :], slot2f[:, :, :]).then_inc(slots_done, 1)
            t_by_e = [P, NT, NE - 1]
            after(dve.tensor_tensor(past[:, :, 0:NE - 1], iotatf[:, 0:NT].unsqueeze(2).broadcast_to(t_by_e),
                                    tiles_to[:, 0:NE - 1].unsqueeze(1).broadcast_to(t_by_e), ALU.is_ge))
            after(dve.tensor_reduce(etf[:, :], past[:, :, 0:NE - 1], AX.X, ALU.add))
            dve.tensor_copy(tiles_to_i[:, :], tiles_to[:, :])
            dve.tensor_copy(et[:, :], etf[:, :]).then_inc(plan_done, 1)
            dve.wait_ge(plan_done, 1)
            dve.wait_ge(loaded_bias, 48)

            def bias_at(t, table, n):
                e = dve.value_load(et[0:1, bass.ds(t, 1)], min_val=0, max_val=NE - 1)
                return table[:, bass.ds(e * n, n)]

            def low(dst, src, high_part, done):
                dve.tensor_tensor(dst, src, high_part.bitcast(F32), ALU.subtract).then_inc(done, 1)

            def step(t, par, half):
                if exists(t):
                    bias = bias_at(t, B2, HF)
                    dve.wait_ge(l2_done, of(l2_done, t + 1))
                    dve.wait_ge(h2_turned, of(h2_turned, t - 1))
                    dve.tensor_tensor(a2[par][:, :], bank[4][:, :], bias, ALU.add).then_inc(a2_done, 1)
                if exists(t - 1):
                    bias = bias_at(t - 1, B3, DM)
                    dve.wait_ge(l3_done, of(l3_done, t))
                    dve.wait_ge(stored_y[1 - par], 16 * (half + (par - 1) // 2))
                    dve.tensor_tensor(yt[1 - par][:, :], bank[5][:, 0:DM], bias, ALU.add).then_inc(y_done, 1)
                if exists(t + 1):
                    dve.wait_ge(h1h_done, of(h1h_done, t + 2))
                    dve.wait_ge(l2_done, of(l2_done, t + 1))
                    low(h1l[:, :, :], bank[1][:, :].rearrange("p (k s) -> p k s", k=KF), h1h[:, :, :], h1l_done)
                if exists(t):
                    dve.wait_ge(h2h_done, of(h2h_done, t + 1))
                    dve.wait_ge(l3_done, of(l3_done, t))
                    low(h2l[:, :, :], bank[2][:, :].rearrange("p (k s) -> p k s", k=KF), h2h[:, :, :], h2l_done)
                if exists(t + 3):
                    dve.wait_ge(xh_done, of(xh_done, t + 4))
                    dve.wait_ge(l1_done, of(l1_done, t + 2))
                    low(xl[1 - par][:, :, :], bank[0][:, 0:DM].rearrange("p (c s) -> p c s", c=2), xh[1 - par][:, :, :], xl_done)
                if exists(t + 2):
                    bias = bias_at(t + 2, B1, HF)
                    dve.wait_ge(l1_done, of(l1_done, t + 3))
                    dve.wait_ge(h1_turned, of(h1_turned, t + 1))
                    dve.tensor_tensor(a1[par][:, :], bank[3][:, :], bias, ALU.add).then_inc(a1_done, 1)

            run_steps(dve, step)
            for b in range(NB):
                dve.wait_ge(gathered[b % 2], 32 * (b // 2 + 1))
                after(dve.scalar_tensor_tensor(out=X[:, b, :], in0=gy[b % 2][:, 0, :], scalar=wtok[:, b, 0:1], in1=X[:, b, :],
                                               op0=ALU.mult, op1=ALU.add))
                dve.scalar_tensor_tensor(out=X[:, b, :], in0=gy[b % 2][:, 1, :], scalar=wtok[:, b, 1:2], in1=X[:, b, :],
                                         op0=ALU.mult, op1=ALU.add).then_inc(final_done, 1)


def kernel(**inputs):
    import numpy as np
    import concourse.bacc as bacc
    from concourse.bass_utils import run_bass_kernel_spmd

    a = {k: np.asarray(v) for k, v in inputs.items()}
    ctx = a["ctx_2048"]
    nb, s, d = ctx.shape
    ctx_t = ctx.transpose(0, 2, 1)
    halves = np.zeros((128, 2), np.float32)
    halves[np.arange(128) % 32 < 16, 0] = 0.25
    halves[np.arange(128) % 32 >= 16, 1] = 0.25
    arrays = {
        "x": a["x"],
        "ctx_2048": ctx,
        "ctx_t": ctx_t,
        "ctx_t_rev": ctx_t.reshape(nb, d // 128, 128, s)[:, :, ::-1].reshape(nb, d, s),
        "g_xattn": a["g_xattn"],
        "g_ffn": a["g_ffn"],
        "lora_w": np.concatenate([a["L0_ffn_router_W"].T, a["L0_ffn_A"].T, a["L0_ffn_base_W"].T], axis=1),
        "lora_bt": a["L0_ffn_B"].T,
        "lora_biases": a["L0_ffn_biases"],
        "ssm_kernel": a["L1_xattn_ssm_kernel"],
        "ssm_d": a["L1_xattn_D"],
        "w1": a["L1_ffn_W1"],
        "w2": a["L1_ffn_W2"],
        "w3": a["L1_ffn_W3"],
        "b1": a["L1_ffn_b1"],
        "b2": a["L1_ffn_b2"],
        "b3": a["L1_ffn_b3"],
        "wg": a["L1_ffn_Wg"],
        "bg": a["L1_ffn_bg"],
        "head_halves": halves,
    }
    nc = bacc.Bacc("TRN2", target_bir_lowering=False, num_devices=1)
    feed, args = {}, {}
    for name, v in arrays.items():
        v = np.ascontiguousarray(v)
        feed[f"in_{name}"] = v
        args[name] = nc.dram_tensor(f"in_{name}", v.shape, mybir.dt.from_np(v.dtype), kind="ExternalInput").ap()
    result = nc.dram_tensor("result", a["x"].shape, mybir.dt.float32, kind="ExternalOutput").ap()
    flamingo_two_layers(nc, out=result, **args)
    r = run_bass_kernel_spmd(nc, [feed], core_ids=[0])
    return r.results[0]["result"]
```

```python
from contextlib import ExitStack

import concourse.bass as bass
from concourse import mybir

F32 = mybir.dt.float32
F32R = mybir.dt.float32r
BF16 = mybir.dt.bfloat16
I32 = mybir.dt.int32
U32 = mybir.dt.uint32
ALU = mybir.AluOpType
ACT = mybir.ActivationFunctionType
AX = mybir.AxisListType

P = 128
EPS = 1e-5
MASKED = -1e30
TAKEN = -3e38


def flamingo_two_layers(nc, x, ctx_2048, ctx_t, ctx_t_rev, g_xattn, g_ffn, lora_w, lora_bt, lora_biases,
                        ssm_kernel, ssm_d, w1, w2, w3, b1, b2, b3, wg, bg, head_halves, out):
    NB, S, DM = x.shape
    assert S == P and DM == 2 * P
    NH, HD = 16, DM // 16
    G = 4
    NG = NH // G
    NR = lora_biases.shape[0]
    NRT = NR // 2
    TOP = 8
    CH = ssm_d.shape[0]
    CD = P // CH
    L = DM
    NE, _, HF = w1.shape
    KF = HF // P
    NT = (2 * NB * S - NE) // P + NE
    SCALING = 2
    OH = 32

    sorted_x = nc.dram_tensor("sorted_x", [NT * P, DM], F32, kind="Internal").ap()
    sorted_y = nc.dram_tensor("sorted_y", [NT * P, DM], F32, kind="Internal").ap()
    kernels = nc.dram_tensor("kernels", [CH, P - 1 + L], F32, kind="Internal").ap()

    with ExitStack() as ctx:
        def sb(name, shape, dt=F32):
            return ctx.enter_context(nc.sbuf_tensor(name, shape, dt))

        def sem(name):
            return ctx.enter_context(nc.semaphore(name))

        X = sb("X", [P, NB, DM])
        HN = sb("HN", [P, NB, DM])
        B1 = sb("B1", [P, NE * HF])
        B2 = sb("B2", [P, NE * HF])
        B3 = sb("B3", [P, NE * DM])
        raw1 = sb("raw1", [P, 2, HF])
        raw2 = sb("raw2", [P, KF, HF])
        raw3 = sb("raw3", [P, KF, DM])
        ident = sb("ident", [P, P])
        identb = sb("identb", [P, P], BF16)
        anti = sb("anti", [P, P])
        causal = sb("causal", [P, G, P], BF16)
        before = sb("before", [P, P], BF16)
        ones = sb("ones", [P, P], BF16)
        halves = sb("halves", [P, 2])
        gates = sb("gates", [P, 4])
        tg = sb("tg", [P, 4])
        lbias = sb("lbias", [P, NR])
        bgb = sb("bgb", [P, NE])
        wg_sb = sb("wg_sb", [P, 2, NE])
        stats = sb("stats", [P, NB, 6])
        mv = sb("mv", [P, NB, 2])
        ve = sb("ve", [P, NB])
        rstd = sb("rstd", [P, NB])
        minus_half = sb("minus_half", [P, NB])
        zeros = sb("zeros", [P, 2048])
        gl = sb("gl", [P, NB, NE])
        gmax = sb("gmax", [P, NB])
        gsum = sb("gsum", [P, NB])
        grec = sb("grec", [P, NB])
        top8 = sb("top8", [P, NB, 8])
        tidx = sb("tidx", [P, NB, 8], U32)
        tidf = sb("tidf", [P, NB, 8])
        wtok = sb("wtok", [P, NB, 2])
        pace = sb("pace", [P, 1])
        iota8 = sb("iota8", [P, NE], I32)
        iota8f = sb("iota8f", [P, NE])
        iota_rows = sb("iota_rows", [P, NE], I32)
        iota_rowsf = sb("iota_rowsf", [P, NE])
        iotat = sb("iotat", [P, 32], I32)
        iotatf = sb("iotatf", [P, 32])
        hot = sb("hot", [P, 2, NB, NE])
        chosen = sb("chosen", [P, NB, NE], BF16)
        over = sb("over", [P, NE, NE])
        tiles_of = sb("tiles_of", [P, NE])
        tiles_to = sb("tiles_to", [P, NE])
        onesr = sb("onesr", [P, NE])
        first_slot = sb("first_slot", [P, NE])
        rank = sb("rank", [P, NB, NE])
        slotf = sb("slotf", [P, NB, NE])
        pick = sb("pick", [P, 2, NB, NE])
        slot2f = sb("slot2f", [P, 2, NB])
        slot2 = sb("slot2", [P, 2, NB], I32)
        past = sb("past", [P, NT, NE])
        etf = sb("etf", [P, NT])
        et = sb("et", [P, NT], I32)
        tiles_to_i = sb("tiles_to_i", [P, NE], I32)

        early = ExitStack()

        def se(name, shape, dt=F32):
            return early.enter_context(nc.sbuf_tensor(name, shape, dt))

        C = se("C", [P, NB, DM])
        ct = [se(f"ct{p}", [P, 2, P]) for p in range(2)]
        va = [se(f"va{p}", [P, NH, OH]) for p in range(2)]
        xn = [se(f"xn{p}", [P, DM]) for p in range(2)]
        qh = [[se(f"qh{p}{o}", [P, 2, P]) for o in range(2)] for p in range(2)]
        pr = [se(f"pr{p}", [P, G, P]) for p in range(2)]
        pt = [se(f"pt{p}", [P, G, P]) for p in range(2)]
        rsum = se("rsum", [P, NH])
        mx = se("mx", [P, 2, G])
        os_ = se("os", [P, NG, P])
        on = se("on", [P, DM])
        HT = se("HT", [P, NB, 2, P])
        LW = se("LW", [P, 2, NRT + NR + DM])
        LB = se("LB", [NR, DM])
        sc = se("sc", [P, NB, NR])
        sg = se("sg", [P, NB, NRT])
        rep = se("rep", [P, NB, NR])
        m8 = se("m8", [P, NB, TOP])
        s8 = se("s8", [P, NB])
        r8 = se("r8", [P, NB])
        mg = se("mg", [P, NB, NR])
        mgT = se("mgT", [NR, NB, P])
        kp = se("kp", [CH, P - 1 + L])
        dcol = se("dcol", [CH, 1])
        CT = se("CT", [P, 2, NB, P])
        QT = se("QT", [P, 2, NB, P])
        us = [se(f"us{p}", [P, L]) for p in range(2)]
        kv = [se(f"kv{p}", [P, 2, NB, CD * CD]) for p in range(2)]
        z = [se(f"z{p}", [P, NB, CD * CD]) for p in range(2)]
        YO = se("YO", [P, 2, NB, P])
        early.close()

        s1h = sb("s1h", [P, 2, 2, HF], F32R)
        s1l = sb("s1l", [P, 2, 2, HF], F32R)
        s2h = sb("s2h", [P, 2, KF, HF], F32R)
        s2l = sb("s2l", [P, 2, KF, HF], F32R)
        s3h = sb("s3h", [P, 2, KF, DM], F32R)
        s3l = sb("s3l", [P, 2, KF, DM], F32R)
        xg = [sb(f"xg{p}", [P, DM]) for p in range(2)]
        xh = [sb(f"xh{p}", [P, 2, P], F32R) for p in range(2)]
        xl = [sb(f"xl{p}", [P, 2, P], F32R) for p in range(2)]
        a1 = [sb(f"a1{p}", [P, HF]) for p in range(2)]
        a2 = [sb(f"a2{p}", [P, HF]) for p in range(2)]
        h1h = sb("h1h", [P, KF, P], F32R)
        h1l = sb("h1l", [P, KF, P], F32R)
        h2h = sb("h2h", [P, KF, P], F32R)
        h2l = sb("h2l", [P, KF, P], F32R)
        yt = [sb(f"yt{p}", [P, DM]) for p in range(2)]
        gy = [sb(f"gy{p}", [P, 2, DM]) for p in range(2)]

        bank = [ctx.enter_context(nc.psum_tensor(f"bank{i}", [P, 512], F32)) for i in range(8)]

        loaded_x = sem("loaded_x")
        loaded_c = sem("loaded_c")
        loaded_ct = [sem("loaded_ct0"), sem("loaded_ct1")]
        loaded_small = sem("loaded_small")
        loaded_lora = sem("loaded_lora")
        loaded_ctx_rev = sem("loaded_ctx_rev")
        loaded_bias = sem("loaded_bias")
        loaded_u = [sem("loaded_u0"), sem("loaded_u1")]
        loaded_w = [sem("loaded_w1"), sem("loaded_w2"), sem("loaded_w3")]
        cleared = sem("cleared")
        consts = sem("consts")
        pool_step = sem("pool_step")
        dve_step = sem("dve_step")
        tanh_done = sem("tanh_done")
        var_done = sem("var_done")
        rstd_done = sem("rstd_done")
        xn_done = sem("xn_done")
        q_turned = sem("q_turned")
        qh_done = sem("qh_done")
        va_done = sem("va_done")
        scores_done = sem("scores_done")
        max_done = sem("max_done")
        shifted = sem("shifted")
        out_step = sem("out_step")
        probs_done = sem("probs_done")
        p_turned = sem("p_turned")
        pt_done = sem("pt_done")
        pv_done = sem("pv_done")
        os_done = sem("os_done")
        o_turned = sem("o_turned")
        attn_done = sem("attn_done")
        normed = sem("normed")
        h_turned = sem("h_turned")
        ht_done = sem("ht_done")
        routed = sem("routed")
        sig_done = sem("sig_done")
        gated = sem("gated")
        g_turned = sem("g_turned")
        mgt_done = sem("mgt_done")
        ffn_done = sem("ffn_done")
        x2_done = sem("x2_done")
        kv_done = sem("kv_done")
        conv_done = sem("conv_done")
        z_done = sem("z_done")
        yo_done = sem("yo_done")
        y_turned = sem("y_turned")
        x3_done = sem("x3_done")
        logits_done = sem("logits_done")
        gexp_done = sem("gexp_done")
        gshift_done = sem("gshift_done")
        chosen_done = sem("chosen_done")
        counted = sem("counted")
        slots_done = sem("slots_done")
        plan_done = sem("plan_done")
        scattered = sem("scattered")
        loaded_xg = [sem("loaded_xg0"), sem("loaded_xg1")]
        x_turned = sem("x_turned")
        xh_done = sem("xh_done")
        xl_done = sem("xl_done")
        l1_done = sem("l1_done")
        l2_done = sem("l2_done")
        l3_done = sem("l3_done")
        a1_done = sem("a1_done")
        a2_done = sem("a2_done")
        g1_done = sem("g1_done")
        g2_done = sem("g2_done")
        h1_turned = sem("h1_turned")
        h2_turned = sem("h2_turned")
        h1h_done = sem("h1h_done")
        h1l_done = sem("h1l_done")
        h2h_done = sem("h2h_done")
        h2l_done = sem("h2l_done")
        y_done = sem("y_done")
        stored_y = [sem("stored_y0"), sem("stored_y1")]
        kernel_row = sem("kernel_row")
        kernels_stored = sem("kernels_stored")
        split_w = [sem("split_w1"), sem("split_w2"), sem("split_w3")]
        gathered = [sem("gathered0"), sem("gathered1")]
        final_done = sem("final_done")
        stored_out = [sem("stored_out0"), sem("stored_out1")]

        CREDIT = 8
        by_dve = (xn_done, shifted, attn_done, z_done, a1_done, a2_done, xl_done, h1l_done, h2l_done, y_done, final_done)
        by_act = (os_done, qh_done, probs_done, pt_done, g1_done, g2_done, xh_done, h1h_done, h2h_done)
        by_pe = (o_turned, q_turned, scores_done, p_turned, pv_done, conv_done, l1_done, l2_done, l3_done, x_turned,
                 h1_turned, h2_turned)
        by_pool = (va_done, kv_done)
        ringed = {s.name for s in by_dve + by_act + by_pe + by_pool}

        def of(s, n):
            assert s.name in ringed
            return n + CREDIT

        def give_credit(eng, sems):
            for s in sems:
                eng.sem_inc(s, CREDIT)

        GROUPS = NB * NG

        def run_groups(eng, step):
            for t in range(-NG, NG):
                step(t, t % (2 * NG), t // NG)
            with eng.Fori(0, (NB - 2) // 2) as i:
                for q in range(NG, 3 * NG):
                    step(i * 2 * NG + q, q % (2 * NG), i * 2 + q // NG)
            for t in range(GROUPS - NG, GROUPS + NG + 1):
                step(t, t % (2 * NG), t // NG)

        def within(t, n):
            return not isinstance(t, int) or 0 <= t < n

        FULL = 1
        PAIRS = (NT - 4) // 2

        def run_steps(eng, step):
            for t in range(-4, FULL):
                step(t, t % 2, t // 2)
            with eng.Fori(0, PAIRS) as i:
                for q in range(FULL, FULL + 2):
                    step(i * 2 + q, q % 2, i + q // 2)
            for t in range(FULL + 2 * PAIRS, NT + 1):
                step(t, t % 2, t // 2)

        def exists(t):
            return not isinstance(t, int) or 0 <= t < NT

        block = ctx.enter_context(nc.Block())

        def to_all(ap, n):
            return bass.AP(ap.tensor, ap.offset, [[0, P], [1, n]])

        N_SMALL = 7
        N_CLEAR = -(-NT * DM // 2048)

        @block.sync
        def _(sp):
            sp.dma_start(X[:, :, :], x.rearrange("b p d -> p b d")).then_inc(loaded_x, 16)
            sp.dma_start(halves[:, :], head_halves).then_inc(loaded_small, 16)
            sp.dma_start(gates[:, 0:2], to_all(g_xattn, 2)).then_inc(loaded_small, 16)
            sp.dma_start(gates[:, 2:4], to_all(g_ffn, 2)).then_inc(loaded_small, 16)
            sp.dma_start(C[:, :, :], ctx_2048.rearrange("b p d -> p b d")).then_inc(loaded_c, 16)
            sp.dma_start(lbias[:, :], to_all(lora_biases, NR)).then_inc(loaded_small, 16)
            sp.dma_start(bgb[:, :], to_all(bg, NE)).then_inc(loaded_small, 16)
            sp.dma_start(wg_sb[:, :, :], wg.rearrange("(c p) n -> p c n", p=P)).then_inc(loaded_small, 16)
            sp.dma_start(LB[:, :], lora_bt).then_inc(loaded_small, 16)
            with sp.Fori(0, NB // 2) as i:
                for p in range(2):
                    sp.wait_ge(scores_done, of(scores_done, i * 2 * NG + (p * NG - NG)))
                    src = ctx_t[bass.ds(2 * i + p, 1), :, :].rearrange("o (c p) s -> p (o c) s", p=P)
                    sp.dma_start(ct[p][:, :, :], src).then_inc(loaded_ct[p], 16)
            sp.dma_start(LW[:, :, :], lora_w.rearrange("(c p) n -> p c n", p=P)).then_inc(loaded_lora, 16)
            for b in range(NB):
                sp.dma_start(CT[:, :, b, :], ctx_t_rev[b].rearrange("(c p) s -> p c s", p=P)).then_inc(loaded_ctx_rev, 16)
            sp.wait_ge(consts, 1)
            sp.dma_start(kp[:, P - 1:P - 1 + L], ssm_kernel).then_inc(kernel_row, 16)
            sp.dma_start(dcol[:, :], ssm_d.rearrange("(h o) -> h o", o=1)).then_inc(kernel_row, 16)
            rows = sorted_x.rearrange("(t p) d -> p t d", p=P)
            for t in range(0, NT, 2048 // DM):
                n = min(2048 // DM, NT - t)
                sp.dma_start(rows[:, t:t + n, :], zeros[:, 0:n * DM].rearrange("p (t d) -> p t d", d=DM)).then_inc(cleared, 16)
            sp.dma_start(B1[:, :], to_all(b1, NE * HF)).then_inc(loaded_bias, 16)
            sp.dma_start(B2[:, :], to_all(b2, NE * HF)).then_inc(loaded_bias, 16)
            sp.dma_start(B3[:, :], to_all(b3, NE * DM)).then_inc(loaded_bias, 16)
            sp.wait_ge(kernel_row, 33)
            sp.dma_start(kernels, kp[:, :]).then_inc(kernels_stored, 16)
            sp.wait_ge(kernels_stored, 16)
            with sp.Fori(0, CH // 2) as i:
                for p in range(2):
                    sp.wait_ge(conv_done, of(conv_done, i * 4 + (2 * p - 2)))
                    src = bass.AP(kernels.tensor, (2 * i + p) * (P - 1 + L), [[1, P], [1, L]])
                    sp.dma_start(us[p][:, :], src).then_inc(loaded_u[p], 16)
            sp.wait_ge(scattered, 16 * 2 * NB)

            def step(t, par, half):
                if exists(t + 4):
                    sp.wait_ge(x_turned, of(x_turned, t + 3))
                    sp.dma_start(xg[par][:, :], sorted_x[bass.ts(t + 4, P), :]).then_inc(loaded_xg[par], 16)
                if exists(t - 1):
                    sp.wait_ge(y_done, of(y_done, t))
                    sp.dma_start(sorted_y[bass.ts(t - 1, P), :], yt[1 - par][:, :]).then_inc(stored_y[1 - par], 16)

            run_steps(sp, step)
            for b in range(NB):
                sp.wait_ge(final_done, of(final_done, b + 1))
                sp.dma_start(out[b], X[:, b, :]).then_inc(stored_out[b % 2], 16)
            for p in range(2):
                sp.wait_ge(stored_out[p], 16 * NB // 2)

        @block.gpsimd
        def _(pool):
            give_credit(pool, by_pool)
            n_after = [0]

            def after(ins):
                n_after[0] += 1
                ins.then_inc(pool_step, 1)
                pool.wait_ge(pool_step, n_after[0])

            pool.memset(kp[:, :], 0.0)
            pool.memset(zeros[:, :], 0.0).then_inc(consts, 1)
            pool.memset(minus_half[:, :], -0.5)
            pool.memset(onesr[:, :], 1.0)
            pool.memset(ident[:, :], 0.0)
            pool.memset(identb[:, :], 0.0)
            pool.memset(causal[:, :, :], 0.0)
            pool.memset(ones[:, :], 1.0)
            for p in range(2):
                pool.memset(va[p][:, :, HD:OH], 0.0)
            after(pool.memset(before[:, :], 1.0))
            for p in range(2):
                pool.memset(va[p][:, :, HD:HD + 1], 1.0)
            pool.affine_select(out=ident[:, :], in_=ident[:, :], compare_op=ALU.not_equal, fill=1.0, base=0,
                               pattern=[[-1, P]], channel_multiplier=1)
            pool.affine_select(out=identb[:, :], in_=identb[:, :], compare_op=ALU.not_equal, fill=1.0, base=0,
                               pattern=[[-1, P]], channel_multiplier=1)
            pool.affine_select(out=causal[:, :, :], in_=causal[:, :, :], compare_op=ALU.is_ge, fill=MASKED, base=0,
                               pattern=[[0, G], [-1, P]], channel_multiplier=1)
            pool.affine_select(out=before[:, :], in_=before[:, :], compare_op=ALU.is_gt, fill=0.0, base=0,
                               pattern=[[1, P]], channel_multiplier=-1)
            pool.iota(iota8[:, :], pattern=[[1, NE]], base=0, channel_multiplier=0)
            pool.iota(iota_rows[:, :], pattern=[[P, NE]], base=0, channel_multiplier=0)
            pool.iota(iotat[:, :], pattern=[[1, 32]], base=0, channel_multiplier=0).then_inc(consts, 1)

            for raw, w, loaded in ((raw1, w1, loaded_w[0]), (raw2, w2, loaded_w[1]), (raw3, w3, loaded_w[2])):
                pool.dma_start(raw[:, :, :], w[0].rearrange("(c p) n -> p c n", p=P)).then_inc(loaded, 16)

            norms = [0]

            def inverse_deviation():
                norms[0] += 1
                pool.wait_ge(var_done, norms[0])
                pool.tensor_tensor(rstd[:, :], ve[:, :], minus_half[:, :], ALU.pow).then_inc(rstd_done, 1)

            inverse_deviation()
            with pool.Fori(0, NB // 2) as i:
                for p in range(2):
                    pool.wait_ge(pv_done, of(pv_done, i * 2 * NG + (p * NG - NG)))
                    pool.wait_ge(loaded_c, 16)
                    src = C[:, bass.ds(2 * i + p, 1), :].rearrange("p o (h d) -> p (o h) d", d=HD)
                    pool.tensor_copy(va[p][:, :, 0:HD], src).then_inc(va_done, 1)
            inverse_deviation()
            inverse_deviation()
            pool.wait_ge(loaded_ctx_rev, 16 * NB)
            with pool.Fori(0, CH // 2) as i:
                for p in range(2):
                    pool.wait_ge(conv_done, of(conv_done, i * 4 + (2 * p - 2)))
                    for c in range(2):
                        kk = CT[:, c, :, bass.ds((2 * i + p) * CD, CD)]
                        o = kv[p][:, c, :, :].rearrange("p b (i j) -> p b i j", j=CD)
                        shape = [P, NB, CD, CD]
                        pool.tensor_tensor(o, kk.unsqueeze(3).broadcast_to(shape), kk.unsqueeze(2).broadcast_to(shape),
                                           ALU.mult).then_inc(kv_done, 1)
            inverse_deviation()

            pool.wait_ge(cleared, 16 * N_CLEAR)
            pool.wait_ge(slots_done, 1)
            for b in range(NB):
                for k in range(2):
                    pool.indirect_dma_start(out=sorted_x, out_offset=bass.IndirectOffsetOnAxis(ap=slot2[:, k, b:b + 1], axis=0),
                                            in_=HN[:, b, :], in_offset=None).then_inc(scattered, 16)

            parts = ((raw1, s1h, s1l, loaded_w[0], split_w[0]), (raw2, s2h, s2l, loaded_w[1], split_w[1]),
                     (raw3, s3h, s3l, loaded_w[2], split_w[2]))

            def split(e, k):
                raw, high, low, loaded, done = parts[k]
                pool.wait_ge(loaded, (e + 1) * 16)
                pool.tensor_scalar(high[:, e % 2, :, :], raw[:, :, :], 1.0, 1.0, ALU.mult, ALU.mult).then_inc(done, 1)
                pool.wait_ge(done, 2 * e + 1)
                pool.tensor_tensor(low[:, e % 2, :, :], raw[:, :, :], high[:, e % 2, :, :].bitcast(F32),
                                   ALU.subtract).then_inc(done, 1)
                if e + 1 < NE:
                    pool.wait_ge(done, 2 * e + 2)
                    pool.dma_start(raw[:, :, :], (w1, w2, w3)[k][e + 1].rearrange("(c p) n -> p c n", p=P)).then_inc(loaded, 16)

            for e in range(2):
                for k in range(3):
                    split(e, k)
            pool.wait_ge(plan_done, 1)
            for e in range(2, NE):
                last = pool.value_load(tiles_to_i[0:1, e - 2:e - 1], min_val=1, max_val=NT)
                for k, passed in enumerate((l1_done, l2_done, l3_done)):
                    pool.wait_ge(passed, of(passed, last))
                    pool.tensor_tensor(pace[:, :], onesr[:, 0:1], onesr[:, 0:1], ALU.mult)
                    split(e, k)
            for p in range(2):
                pool.wait_ge(stored_y[p], 16 * ((NT + 1 - p) // 2))
            for b in range(NB):
                pool.wait_ge(final_done, of(final_done, b - 1))
                for k in range(2):
                    pool.indirect_dma_start(out=gy[b % 2][:, k, :], out_offset=None, in_=sorted_y,
                                            in_offset=bass.IndirectOffsetOnAxis(ap=slot2[:, k, b:b + 1], axis=0)
                                            ).then_inc(gathered[b % 2], 16)

        @block.tensor
        def _(pe):
            give_credit(pe, by_pe)
            TQ, TO, SB, PTB, OB = bank[0], bank[1], bank[2:4], bank[4:6], bank[6:8]
            pe.wait_ge(consts, 2)

            def step(t, n, b):
                p, r = n // NG, n % NG
                if r == 1 and within(b + 1, NB):
                    pe.wait_ge(xn_done, of(xn_done, b + 2))
                    pe.wait_ge(qh_done, of(qh_done, b * 2 + 2))
                    for c in range(2):
                        last = pe.transpose(TQ[:, c * P:(c + 1) * P], xn[1 - p][:, c * P:(c + 1) * P], ident[:, :])
                    last.then_inc(q_turned, 1)
                if within(t, GROUPS):
                    if r == 0:
                        pe.wait_ge(loaded_ct[p], 16 * (b // 2 + 1) if isinstance(b, int) else b * 8 + (16 - 8 * p))
                        pe.wait_ge(qh_done, of(qh_done, b * 2 + 2))
                    pe.wait_ge(shifted, of(shifted, t - 1))
                    o = SB[n % 2]
                    pe.matmul(o[:, :], identb[:, :], causal[:, :, :].rearrange("p g k -> p (g k)"), start=True, stop=False,
                              skip_group_check=True)
                    for j in range(G):
                        c, odd = j // 2, j % 2
                        last = pe.matmul(o[:, j * P:(j + 1) * P], qh[p][odd][32 * r:32 * r + 32, c, :],
                                         ct[p][32 * r:32 * r + 32, c, :], start=False, stop=(j == G - 1), skip_group_check=True)
                    last.then_inc(scores_done, 1)
                if within(t - 2, GROUPS):
                    pe.wait_ge(probs_done, of(probs_done, t - 1))
                    pe.wait_ge(pt_done, of(pt_done, t - 3))
                    for j in range(G):
                        last = pe.transpose(PTB[n % 2][:, j * P:(j + 1) * P], pr[n % 2][:, j, :], ident[:, :])
                    last.then_inc(p_turned, 1)
                if within(t - 3, GROUPS):
                    m = (n - 3) % (2 * NG)
                    pm, rm = m // NG, m % NG
                    if rm == 0:
                        pe.wait_ge(va_done, of(va_done, b + 1))
                        pe.wait_ge(os_done, of(os_done, b - 1))
                    pe.wait_ge(pt_done, of(pt_done, t - 2))
                    for j in range(G):
                        h = 8 * (j // 2) + 2 * rm + j % 2
                        last = pe.matmul(OB[pm][32 * j:32 * j + 32, rm * P:(rm + 1) * P], va[pm][:, h, :], pt[m % 2][:, j, :],
                                         start=True, stop=True, skip_group_check=True)
                    last.then_inc(pv_done, 1)
                if r == 3 and within(b - 1, NB):
                    pe.wait_ge(os_done, of(os_done, b))
                    pe.wait_ge(attn_done, of(attn_done, b - 1))
                    for k in range(NG):
                        last = pe.transpose(TO[:, k * P:(k + 1) * P], os_[:, k, :], ident[:, :])
                    last.then_inc(o_turned, 1)

            run_groups(pe, step)

            pairs = [0]

            def turn_norm(banks):
                first = 2 * pairs[0]
                for b in range(NB):
                    pe.wait_ge(normed, first + b + 1)
                    if b >= 4 and b % 2 == 0:
                        pe.wait_ge(ht_done, pairs[0] - 1)
                    for c in range(2):
                        last = pe.transpose(banks[(b // 2) % 2][:, (2 * (b % 2) + c) * P:(2 * (b % 2) + c + 1) * P],
                                            HN[:, b, c * P:(c + 1) * P], ident[:, :])
                    if b % 2:
                        pairs[0] += 1
                        last.then_inc(h_turned, 1)

            turn_norm(bank[0:2])
            pe.wait_ge(loaded_lora, 16)
            pe.wait_ge(loaded_small, 16 * N_SMALL)
            pe.wait_ge(attn_done, of(attn_done, NB))
            NW = NRT + NR
            for b in range(NB):
                if b % 2 == 0:
                    pe.wait_ge(ht_done, b // 2 + 1)
                for c in range(2):
                    last = pe.matmul(bank[2 + b // 4][:, (b % 4) * P:(b % 4) * P + NW], HT[:, b, c, :], LW[:, c, 0:NW],
                                     start=(c == 0), stop=(c == 1), skip_group_check=True)
                if b % 4 == 3:
                    last.then_inc(routed, 1)
            for b in range(NB):
                pe.wait_ge(gated, b + 1)
                last = pe.transpose(bank[b // 4][0:NR, (b % 4) * P:(b % 4 + 1) * P], mg[:, b, :], ident[:, :])
                if b % 4 == 3:
                    last.then_inc(g_turned, 1)
            for b in range(NB):
                o = bank[4 + b // 2][:, (b % 2) * DM:(b % 2 + 1) * DM]
                for c in range(2):
                    pe.matmul(o, HT[:, b, c, :], LW[:, c, NW:NW + DM], start=(c == 0), stop=False, skip_group_check=True)
                if b % 4 == 0:
                    pe.wait_ge(mgt_done, b // 4 + 1)
                last = pe.matmul(o, mgT[:, b, :], LB[:, :], start=False, stop=True, skip_group_check=True)
                if b % 2:
                    last.then_inc(ffn_done, 1)

            turn_norm(bank[0:2])
            pe.wait_ge(x2_done, 1)
            YB = bank[2:6]
            with pe.Fori(0, CH // 2) as i:
                for p in range(2):
                    pe.wait_ge(loaded_u[p], i * 16 + 16)
                    for c in range(2):
                        n = 2 * p + c
                        pe.wait_ge(kv_done, of(kv_done, i * 4 + (n + 1)))
                        pe.wait_ge(z_done, of(z_done, i * 4 + (n - 3)))
                        o = YB[n][:, :]
                        rhs = kv[p][:, :, :, :].rearrange("p c b k -> p c (b k)")
                        if c == 0:
                            last = pe.matmul(o, us[p][:, 0:P], rhs[:, 0, :], start=True, stop=True)
                        else:
                            pe.matmul(o, us[p][:, P:2 * P], rhs[:, 0, :], start=True, stop=False)
                            last = pe.matmul(o, us[p][:, 0:P], rhs[:, 1, :], start=False, stop=True)
                        last.then_inc(conv_done, 1)
            pe.wait_ge(yo_done, 1)
            for b in range(NB):
                if b >= 4:
                    pe.wait_ge(x3_done, b - 3)
                for c in range(2):
                    last = pe.transpose(bank[b % 4][:, c * P:(c + 1) * P], YO[:, c, b, :], ident[:, :])
                last.then_inc(y_turned, 1)

            turn_norm(bank[4:6])
            for b in range(NB):
                if b % 2 == 0:
                    pe.wait_ge(ht_done, 8 + b // 2 + 1)
                for c in range(2):
                    last = pe.matmul(bank[6][:, b * NE:(b + 1) * NE], HT[:, b, c, :], wg_sb[:, c, :],
                                     start=(c == 0), stop=(c == 1), skip_group_check=True)
            last.then_inc(logits_done, 1)
            pe.wait_ge(chosen_done, 1)
            pe.matmul(bank[7][:, 0:NB * NE], before[:, :], chosen[:, :, :].rearrange("p b e -> p (b e)"), start=True,
                      stop=False, skip_group_check=True)
            for b in range(NB - 1):
                for b2 in range(b + 1, NB):
                    pe.matmul(bank[7][:, b2 * NE:(b2 + 1) * NE], ones[:, :], chosen[:, b, :],
                              start=False, stop=(b == NB - 2), skip_group_check=True)
            for b in range(NB):
                last = pe.matmul(bank[4][:, 0:NE], ones[:, :], chosen[:, b, :], start=(b == 0), stop=(b == NB - 1))
            last.then_inc(counted, 1)

            pe.wait_ge(plan_done, 1)

            def expert(t):
                return pe.value_load(et[0:1, bass.ds(t, 1)], min_val=0, max_val=NE - 1)

            def layer(e, k, o, high, low, w_high, w_low, n_k, done):
                pe.wait_ge(split_w[k], e * 2 + 2)
                for j in range(n_k):
                    for m, (a, w) in enumerate(((high, w_high), (high, w_low), (low, w_high))):
                        last = pe.matmul(o, a[:, j, :], w[:, bass.ds(e % 2, 1), j, :].rearrange("p o n -> p (o n)"),
                                         start=(j == 0 and m == 0), stop=(j == n_k - 1 and m == 2))
                last.then_inc(done, 1)

            def turn(o, src, n_k, done):
                for j in range(n_k):
                    last = pe.transpose(o[:, j * P:(j + 1) * P], src[:, j * P:(j + 1) * P], ident[:, :])
                last.then_inc(done, 1)

            def step(t, par, half):
                if exists(t):
                    e = expert(t)
                    pe.wait_ge(h1h_done, of(h1h_done, t + 1))
                    pe.wait_ge(h1l_done, of(h1l_done, t + 1))
                    pe.wait_ge(a2_done, of(a2_done, t))
                    layer(e, 1, bank[4][:, :], h1h, h1l, s2h, s2l, KF, l2_done)
                if exists(t - 1):
                    e = expert(t - 1)
                    pe.wait_ge(h2h_done, of(h2h_done, t))
                    pe.wait_ge(h2l_done, of(h2l_done, t))
                    pe.wait_ge(y_done, of(y_done, t - 1))
                    layer(e, 2, bank[5][:, 0:DM], h2h, h2l, s3h, s3l, KF, l3_done)
                if exists(t + 1):
                    pe.wait_ge(g1_done, of(g1_done, t + 2))
                    pe.wait_ge(h1l_done, of(h1l_done, t + 1))
                    turn(bank[1], a1[1 - par], KF, h1_turned)
                if exists(t):
                    pe.wait_ge(g2_done, of(g2_done, t + 1))
                    pe.wait_ge(h2l_done, of(h2l_done, t))
                    turn(bank[2], a2[par], KF, h2_turned)
                if exists(t + 2):
                    e = expert(t + 2)
                    pe.wait_ge(xh_done, of(xh_done, t + 3))
                    pe.wait_ge(xl_done, of(xl_done, t + 3))
                    pe.wait_ge(a1_done, of(a1_done, t + 2))
                    layer(e, 0, bank[3][:, :], xh[par], xl[par], s1h, s1l, 2, l1_done)
                if exists(t + 3):
                    pe.wait_ge(loaded_xg[1 - par], 16 * (half + (par + 3) // 2 + 1))
                    pe.wait_ge(xl_done, of(xl_done, t + 3))
                    turn(bank[0], xg[1 - par], 2, x_turned)

            run_steps(pe, step)

        @block.scalar
        def _(act):
            give_credit(act, by_act)
            act.wait_ge(loaded_small, 16 * N_SMALL)
            act.activation(tg[:, :], gates[:, :], ACT.Tanh).then_inc(tanh_done, 1)
            def step(t, n, b):
                p, r = n // NG, n % NG
                if within(t, GROUPS):
                    act.wait_ge(shifted, of(shifted, t + 1))
                    act.activation(pr[n % 2][:, :, :], pr[n % 2][:, :, :], ACT.Exp).then_inc(probs_done, 1)
                if r == 1 and within(b + 1, NB):
                    act.wait_ge(q_turned, of(q_turned, b + 2))
                    act.wait_ge(scores_done, of(scores_done, b * NG))
                    for odd in range(2):
                        act.activation(qh[1 - p][odd][:, :, :], bank[0][:, 0:DM].rearrange("p (c s) -> p c s", c=2), ACT.Copy,
                                       scale=halves[:, odd:odd + 1]).then_inc(qh_done, 1)
                if within(t - 2, GROUPS):
                    act.wait_ge(p_turned, of(p_turned, t - 1))
                    act.wait_ge(pv_done, of(pv_done, t - 3))
                    act.activation(pt[n % 2][:, :, :], bank[4 + n % 2][:, :].rearrange("p (g s) -> p g s", g=G),
                                   ACT.Copy).then_inc(pt_done, 1)
                if r == 2 and within(b - 1, NB):
                    act.wait_ge(pv_done, of(pv_done, b * NG))
                    act.wait_ge(o_turned, of(o_turned, b - 1))
                    act.activation(os_[:, :, :], bank[6 + (1 - p)][:, :].rearrange("p (r s) -> p r s", r=NG),
                                   ACT.Copy).then_inc(os_done, 1)

            run_groups(act, step)

            copied = [0]

            def copy_turned(banks, dst):
                for k in range(NB // 2):
                    copied[0] += 1
                    act.wait_ge(h_turned, copied[0])
                    act.activation(dst(k), banks[k % 2][:, :].rearrange("p (b c s) -> p b c s", b=2, c=2),
                                   ACT.Copy).then_inc(ht_done, 1)

            copy_turned(bank[0:2], lambda k: HT[:, 2 * k:2 * k + 2, :, :])
            for k in range(2):
                act.wait_ge(routed, k + 1)
                act.activation(sg[:, 4 * k:4 * k + 4, :], bank[2 + k][:, :].rearrange("p (b n) -> p b n", b=4)[:, :, 0:NRT],
                               ACT.Exp, scale=-1.0).then_inc(sig_done, 1)
            for k in range(2):
                act.wait_ge(g_turned, k + 1)
                act.activation(mgT[:, 4 * k:4 * k + 4, :], bank[k][0:NR, :].rearrange("p (b s) -> p b s", b=4),
                               ACT.Copy).then_inc(mgt_done, 1)
            copy_turned(bank[0:2], lambda k: QT[:, :, 2 * k:2 * k + 2, :].rearrange("p c b s -> p b c s"))
            copy_turned(bank[4:6], lambda k: HT[:, 2 * k:2 * k + 2, :, :])
            act.wait_ge(gshift_done, 1)
            act.activation(gl[:, :, :], gl[:, :, :], ACT.Exp).then_inc(gexp_done, 1)

            def step(t, par, half):
                if exists(t):
                    act.wait_ge(a2_done, of(a2_done, t + 1))
                    act.activation(a2[par][:, :], a2[par][:, :], ACT.Gelu).then_inc(g2_done, 1)
                if exists(t + 1):
                    act.wait_ge(h1_turned, of(h1_turned, t + 2))
                    act.wait_ge(l2_done, of(l2_done, t + 1))
                    act.activation(h1h[:, :, :], bank[1][:, :].rearrange("p (k s) -> p k s", k=KF), ACT.Copy).then_inc(h1h_done, 1)
                if exists(t):
                    act.wait_ge(h2_turned, of(h2_turned, t + 1))
                    act.wait_ge(l3_done, of(l3_done, t))
                    act.activation(h2h[:, :, :], bank[2][:, :].rearrange("p (k s) -> p k s", k=KF), ACT.Copy).then_inc(h2h_done, 1)
                if exists(t + 2):
                    act.wait_ge(a1_done, of(a1_done, t + 3))
                    act.activation(a1[par][:, :], a1[par][:, :], ACT.Gelu).then_inc(g1_done, 1)
                if exists(t + 3):
                    act.wait_ge(x_turned, of(x_turned, t + 4))
                    act.wait_ge(l1_done, of(l1_done, t + 2))
                    act.activation(xh[1 - par][:, :, :], bank[0][:, 0:DM].rearrange("p (c s) -> p c s", c=2),
                                   ACT.Copy).then_inc(xh_done, 1)

            run_steps(act, step)

        @block.vector
        def _(dve):
            give_credit(dve, by_dve)
            n_after = [0]

            def after(ins):
                n_after[0] += 1
                ins.then_inc(dve_step, 1)
                dve.wait_ge(dve_step, n_after[0])

            norms = [0]

            def deviations():
                for b in range(NB):
                    ins = dve.bn_stats(stats[:, b, :], X[:, b, :])
                after(ins)
                for b in range(NB):
                    ins = dve.bn_aggr(mv[:, b, :], stats[:, b, :])
                after(ins)
                dve.tensor_scalar(ve[:, :], mv[:, :, 1], EPS, None, ALU.add).then_inc(var_done, 1)
                norms[0] += 1
                dve.wait_ge(rstd_done, norms[0])

            def norm_all():
                deviations()
                for b in range(NB):
                    dve.tensor_scalar(HN[:, b, :], X[:, b, :], mv[:, b, 0:1], rstd[:, b:b + 1], ALU.subtract,
                                      ALU.mult).then_inc(normed, 1)

            dve.wait_ge(loaded_x, 16)
            deviations()

            def step(t, n, b):
                p, r = n // NG, n % NG
                if r == 0 and within(b + 1, NB):
                    dve.wait_ge(q_turned, of(q_turned, b))
                    nb = b + 1
                    dve.tensor_scalar(xn[1 - p][:, :], X[:, bass.ds(nb, 1), :].rearrange("p o d -> p (o d)"),
                                      mv[:, bass.ds(nb, 1), 0:1].rearrange("p o d -> p (o d)"), rstd[:, bass.ds(nb, 1)],
                                      ALU.subtract, ALU.mult).then_inc(xn_done, 1)
                if within(t, GROUPS):
                    dve.wait_ge(scores_done, of(scores_done, t + 1))
                    sg_ = bank[2 + n % 2][:, :].rearrange("p (g k) -> p g k", g=G)
                    dve.tensor_reduce(mx[:, n % 2, :], sg_, AX.X, ALU.max).then_inc(max_done, 1)
                    dve.wait_ge(max_done, t + 1)
                    dve.wait_ge(p_turned, of(p_turned, t - 1))
                    dve.tensor_tensor(pr[n % 2][:, :, :], sg_, mx[:, n % 2, :].unsqueeze(2).broadcast_to([P, G, P]),
                                      ALU.subtract).then_inc(shifted, 1)
                if r == 3 and within(b - 1, NB):
                    def then(k, ins):
                        ins.then_inc(out_step, 1)
                        dve.wait_ge(out_step, (b - 1) * 4 + k)

                    dve.wait_ge(o_turned, of(o_turned, b))
                    o = bank[1][:, :].rearrange("p (r g d) -> p r g d", r=NG, g=G)
                    w = rsum[:, :].rearrange("p (r g) -> p r g", g=G)
                    then(1, dve.reciprocal(w, o[:, :, :, HD]))
                    then(2, dve.tensor_scalar(rsum[:, :], rsum[:, :], tg[:, 0:1], None, ALU.mult))
                    for c in range(2):
                        ins = dve.tensor_tensor(on[:, c * P:(c + 1) * P].rearrange("p (r o d) -> p r o d", o=2, d=HD),
                                                o[:, :, 2 * c:2 * c + 2, 0:HD],
                                                w[:, :, 2 * c:2 * c + 2].unsqueeze(3).broadcast_to([P, NG, 2, HD]), ALU.mult)
                        if c == 0:
                            ins.then_inc(out_step, 1)
                    then(4, ins)
                    xb = X[:, bass.ds(b - 1, 1), :].rearrange("p o d -> p (o d)")
                    dve.tensor_tensor(xb, on[:, :], xb, ALU.add).then_inc(attn_done, 1)

            run_groups(dve, step)
            dve.wait_ge(attn_done, of(attn_done, NB))

            norm_all()
            dve.wait_ge(sig_done, 2)
            after(dve.tensor_scalar(sg[:, :, :], sg[:, :, :], 1.0, None, ALU.add))
            after(dve.reciprocal(sg[:, :, :], sg[:, :, :]))
            shape = [P, NB, NRT, 2]
            after(dve.tensor_tensor(sc[:, :, :].rearrange("p b (n r) -> p b n r", r=2), sg[:, :, :].unsqueeze(3).broadcast_to(shape),
                                    lbias[:, :].rearrange("p (n r) -> p n r", r=2).unsqueeze(1).broadcast_to(shape), ALU.add))
            for b in range(NB):
                ins = dve.max(m8[:, b, :], sc[:, b, :])
            after(ins)
            dve.tensor_reduce(s8[:, :], m8[:, :, :], AX.X, ALU.add)
            for b in range(NB):
                ins = dve.match_replace(rep[:, b, :], m8[:, b, :], sc[:, b, :], TAKEN)
            after(ins)
            after(dve.reciprocal(r8[:, :], s8[:, :]))
            dve.tensor_scalar(r8[:, :], r8[:, :], float(TOP * SCALING), None, ALU.mult)
            after(dve.scalar_tensor_tensor(out=rep[:, :, :], in0=rep[:, :, :], scalar=TAKEN, in1=sc[:, :, :],
                                           op0=ALU.is_equal, op1=ALU.mult))
            for b in range(NB):
                mid = bank[2 + b // 4][:, (b % 4) * P + NRT:(b % 4) * P + NRT + NR]
                dve.scalar_tensor_tensor(out=mg[:, b, :], in0=rep[:, b, :], scalar=r8[:, b:b + 1], in1=mid,
                                         op0=ALU.mult, op1=ALU.mult).then_inc(gated, 1)
            for b in range(NB):
                if b % 2 == 0:
                    dve.wait_ge(ffn_done, b // 2 + 1)
                ins = dve.scalar_tensor_tensor(out=X[:, b, :], in0=bank[4 + b // 2][:, (b % 2) * DM:(b % 2 + 1) * DM],
                                               scalar=tg[:, 2:3], in1=X[:, b, :], op0=ALU.mult, op1=ALU.add)
            ins.then_inc(x2_done, 1)
            dve.wait_ge(x2_done, 1)

            norm_all()
            dve.wait_ge(kernel_row, 32)
            dve.tensor_tensor(kp[:, P - 1:P], kp[:, P - 1:P], dcol[:, :], ALU.add).then_inc(kernel_row, 1)
            dve.wait_ge(ht_done, 8)
            C_STEPS = 4
            first_step2 = n_after[0]
            with dve.Fori(0, CH // 2) as i:
                for n in range(4):
                    p, c = n // 2, n % 2
                    cols = bass.ds((2 * i + p) * CD, CD)
                    dve.wait_ge(conv_done, of(conv_done, i * 4 + (n + 1)))
                    shape = [P, NB, CD, CD]
                    zz = z[n % 2][:, :, :].rearrange("p b (i j) -> p b i j", j=CD)
                    dve.tensor_tensor(zz, bank[2 + n][:, :].rearrange("p (b i j) -> p b i j", b=NB, j=CD),
                                      QT[:, c, :, cols].unsqueeze(3).broadcast_to(shape), ALU.mult).then_inc(z_done, 1)
                    dve.wait_ge(z_done, of(z_done, i * 4 + (n + 1)))
                    dve.tensor_reduce(YO[:, c, :, cols], zz.rearrange("p b i j -> p b j i"), AX.X, ALU.add).then_inc(dve_step, 1)
            n_after[0] = first_step2 + (CH // 2) * C_STEPS
            dve.wait_ge(dve_step, n_after[0])
            dve.tensor_copy(iota8f[:, :], iota8[:, :]).then_inc(yo_done, 1)
            dve.tensor_copy(iota_rowsf[:, :], iota_rows[:, :])
            after(dve.tensor_copy(iotatf[:, :], iotat[:, :]))
            for b in range(NB):
                dve.wait_ge(y_turned, b + 1)
                ins = dve.scalar_tensor_tensor(out=X[:, b, :], in0=bank[b % 4][:, 0:DM], scalar=tg[:, 1:2], in1=X[:, b, :],
                                               op0=ALU.mult, op1=ALU.add).then_inc(x3_done, 1)
            dve.wait_ge(x3_done, NB)

            norm_all()
            dve.wait_ge(logits_done, 1)
            by_e = [P, NB, NE]
            after(dve.tensor_tensor(gl[:, :, :], bank[6][:, 0:NB * NE].rearrange("p (b e) -> p b e", e=NE),
                                    bgb[:, :].unsqueeze(1).broadcast_to(by_e), ALU.add))
            after(dve.tensor_reduce(gmax[:, :], gl[:, :, :], AX.X, ALU.max))
            dve.tensor_tensor(gl[:, :, :], gl[:, :, :], gmax[:, :].unsqueeze(2).broadcast_to(by_e), ALU.subtract).then_inc(gshift_done, 1)
            dve.wait_ge(gexp_done, 1)
            after(dve.tensor_reduce(gsum[:, :], gl[:, :, :], AX.X, ALU.add))
            after(dve.reciprocal(grec[:, :], gsum[:, :]))
            after(dve.tensor_tensor(gl[:, :, :], gl[:, :, :], grec[:, :].unsqueeze(2).broadcast_to(by_e), ALU.mult))
            for b in range(NB):
                ins = dve.max(top8[:, b, :], gl[:, b, :])
            after(ins)
            dve.tensor_scalar(wtok[:, :, :], top8[:, :, 0:2], tg[:, 3:4], None, ALU.mult)
            for b in range(NB):
                ins = dve.max_index(tidx[:, b, :], top8[:, b, :], gl[:, b, :])
            after(ins)
            after(dve.tensor_copy(tidf[:, :, :], tidx[:, :, :]))
            for k in range(2):
                ins = dve.tensor_tensor(hot[:, k, :, :], iota8f[:, :].unsqueeze(1).broadcast_to(by_e),
                                        tidf[:, :, k].unsqueeze(2).broadcast_to(by_e), ALU.is_equal)
            after(ins)
            dve.tensor_tensor(chosen[:, :, :], hot[:, 0, :, :], hot[:, 1, :, :], ALU.add).then_inc(chosen_done, 1)
            dve.wait_ge(counted, 1)
            e_by_j = [P, NE, NE]
            after(dve.tensor_tensor(over[:, :, :], bank[4][:, 0:NE].unsqueeze(2).broadcast_to(e_by_j),
                                    iota_rowsf[:, :].unsqueeze(1).broadcast_to(e_by_j), ALU.is_gt))
            after(dve.tensor_reduce(tiles_of[:, :], over[:, :, :], AX.X, ALU.add))
            after(dve.tensor_scalar(tiles_of[:, :], tiles_of[:, :], 1.0, None, ALU.max))
            after(dve.tensor_tensor_scan(tiles_to[:, :], onesr[:, :], tiles_of[:, :], 0.0, ALU.mult, ALU.add))
            after(dve.tensor_tensor(first_slot[:, :], tiles_to[:, :], tiles_of[:, :], ALU.subtract))
            after(dve.tensor_scalar(first_slot[:, :], first_slot[:, :], float(P), None, ALU.mult))
            after(dve.tensor_tensor(slotf[:, :, :], bank[7][:, 0:NB * NE].rearrange("p (b e) -> p b e", e=NE),
                                    first_slot[:, :].unsqueeze(1).broadcast_to(by_e), ALU.add))
            for k in range(2):
                ins = dve.tensor_tensor(pick[:, k, :, :], hot[:, k, :, :], slotf[:, :, :], ALU.mult)
            after(ins)
            after(dve.tensor_reduce(slot2f[:, :, :], pick[:, :, :, :], AX.X, ALU.add))
            dve.tensor_copy(slot2[:, :, :], slot2f[:, :, :]).then_inc(slots_done, 1)
            t_by_e = [P, NT, NE - 1]
            after(dve.tensor_tensor(past[:, :, 0:NE - 1], iotatf[:, 0:NT].unsqueeze(2).broadcast_to(t_by_e),
                                    tiles_to[:, 0:NE - 1].unsqueeze(1).broadcast_to(t_by_e), ALU.is_ge))
            after(dve.tensor_reduce(etf[:, :], past[:, :, 0:NE - 1], AX.X, ALU.add))
            dve.tensor_copy(tiles_to_i[:, :], tiles_to[:, :])
            dve.tensor_copy(et[:, :], etf[:, :]).then_inc(plan_done, 1)
            dve.wait_ge(plan_done, 1)
            dve.wait_ge(loaded_bias, 48)

            def bias_at(t, table, n):
                e = dve.value_load(et[0:1, bass.ds(t, 1)], min_val=0, max_val=NE - 1)
                return table[:, bass.ds(e * n, n)]

            def low(dst, src, high_part, done):
                dve.tensor_tensor(dst, src, high_part.bitcast(F32), ALU.subtract).then_inc(done, 1)

            def step(t, par, half):
                if exists(t):
                    bias = bias_at(t, B2, HF)
                    dve.wait_ge(l2_done, of(l2_done, t + 1))
                    dve.wait_ge(h2_turned, of(h2_turned, t - 1))
                    dve.tensor_tensor(a2[par][:, :], bank[4][:, :], bias, ALU.add).then_inc(a2_done, 1)
                if exists(t - 1):
                    bias = bias_at(t - 1, B3, DM)
                    dve.wait_ge(l3_done, of(l3_done, t))
                    dve.wait_ge(stored_y[1 - par], 16 * (half + (par - 1) // 2))
                    dve.tensor_tensor(yt[1 - par][:, :], bank[5][:, 0:DM], bias, ALU.add).then_inc(y_done, 1)
                if exists(t + 1):
                    dve.wait_ge(h1h_done, of(h1h_done, t + 2))
                    dve.wait_ge(l2_done, of(l2_done, t + 1))
                    low(h1l[:, :, :], bank[1][:, :].rearrange("p (k s) -> p k s", k=KF), h1h[:, :, :], h1l_done)
                if exists(t):
                    dve.wait_ge(h2h_done, of(h2h_done, t + 1))
                    dve.wait_ge(l3_done, of(l3_done, t))
                    low(h2l[:, :, :], bank[2][:, :].rearrange("p (k s) -> p k s", k=KF), h2h[:, :, :], h2l_done)
                if exists(t + 2):
                    bias = bias_at(t + 2, B1, HF)
                    dve.wait_ge(l1_done, of(l1_done, t + 3))
                    dve.wait_ge(h1_turned, of(h1_turned, t + 1))
                    dve.tensor_tensor(a1[par][:, :], bank[3][:, :], bias, ALU.add).then_inc(a1_done, 1)
                if exists(t + 3):
                    dve.wait_ge(xh_done, of(xh_done, t + 4))
                    dve.wait_ge(l1_done, of(l1_done, t + 2))
                    low(xl[1 - par][:, :, :], bank[0][:, 0:DM].rearrange("p (c s) -> p c s", c=2), xh[1 - par][:, :, :], xl_done)

            run_steps(dve, step)
            for b in range(NB):
                dve.wait_ge(gathered[b % 2], 32 * (b // 2 + 1))
                after(dve.scalar_tensor_tensor(out=X[:, b, :], in0=gy[b % 2][:, 0, :], scalar=wtok[:, b, 0:1], in1=X[:, b, :],
                                               op0=ALU.mult, op1=ALU.add))
                dve.scalar_tensor_tensor(out=X[:, b, :], in0=gy[b % 2][:, 1, :], scalar=wtok[:, b, 1:2], in1=X[:, b, :],
                                         op0=ALU.mult, op1=ALU.add).then_inc(final_done, 1)


def kernel(**inputs):
    import numpy as np
    import concourse.bacc as bacc
    from concourse.bass_utils import run_bass_kernel_spmd

    a = {k: np.asarray(v) for k, v in inputs.items()}
    ctx = a["ctx_2048"]
    nb, s, d = ctx.shape
    ctx_t = ctx.transpose(0, 2, 1)
    halves = np.zeros((128, 2), np.float32)
    halves[np.arange(128) % 32 < 16, 0] = 0.25
    halves[np.arange(128) % 32 >= 16, 1] = 0.25
    arrays = {
        "x": a["x"],
        "ctx_2048": ctx,
        "ctx_t": ctx_t,
        "ctx_t_rev": ctx_t.reshape(nb, d // 128, 128, s)[:, :, ::-1].reshape(nb, d, s),
        "g_xattn": a["g_xattn"],
        "g_ffn": a["g_ffn"],
        "lora_w": np.concatenate([a["L0_ffn_router_W"].T, a["L0_ffn_A"].T, a["L0_ffn_base_W"].T], axis=1),
        "lora_bt": a["L0_ffn_B"].T,
        "lora_biases": a["L0_ffn_biases"],
        "ssm_kernel": a["L1_xattn_ssm_kernel"],
        "ssm_d": a["L1_xattn_D"],
        "w1": a["L1_ffn_W1"],
        "w2": a["L1_ffn_W2"],
        "w3": a["L1_ffn_W3"],
        "b1": a["L1_ffn_b1"],
        "b2": a["L1_ffn_b2"],
        "b3": a["L1_ffn_b3"],
        "wg": a["L1_ffn_Wg"],
        "bg": a["L1_ffn_bg"],
        "head_halves": halves,
    }
    nc = bacc.Bacc("TRN2", target_bir_lowering=False, num_devices=1)
    feed, args = {}, {}
    for name, v in arrays.items():
        v = np.ascontiguousarray(v)
        feed[f"in_{name}"] = v
        args[name] = nc.dram_tensor(f"in_{name}", v.shape, mybir.dt.from_np(v.dtype), kind="ExternalInput").ap()
    result = nc.dram_tensor("result", a["x"].shape, mybir.dt.float32, kind="ExternalOutput").ap()
    flamingo_two_layers(nc, out=result, **args)
    r = run_bass_kernel_spmd(nc, [feed], core_ids=[0])
    return r.results[0]["result"]
```

```python
from contextlib import ExitStack

import concourse.bass as bass
from concourse import mybir

F32 = mybir.dt.float32
F32R = mybir.dt.float32r
BF16 = mybir.dt.bfloat16
I32 = mybir.dt.int32
U32 = mybir.dt.uint32
ALU = mybir.AluOpType
ACT = mybir.ActivationFunctionType
AX = mybir.AxisListType

P = 128
EPS = 1e-5
MASKED = -1e30
TAKEN = -3e38


def flamingo_two_layers(nc, x, ctx_2048, ctx_t, ctx_t_rev, g_xattn, g_ffn, lora_w, lora_bt, lora_biases,
                        ssm_kernel, ssm_d, w1, w2, w3, b1, b2, b3, wg, bg, head_halves, out):
    NB, S, DM = x.shape
    assert S == P and DM == 2 * P
    NH, HD = 16, DM // 16
    G = 4
    NG = NH // G
    NR = lora_biases.shape[0]
    NRT = NR // 2
    TOP = 8
    CH = ssm_d.shape[0]
    CD = P // CH
    L = DM
    NE, _, HF = w1.shape
    KF = HF // P
    NT = (2 * NB * S - NE) // P + NE
    SCALING = 2
    OH = 32

    sorted_x = nc.dram_tensor("sorted_x", [NT * P, DM], F32, kind="Internal").ap()
    sorted_y = nc.dram_tensor("sorted_y", [NT * P, DM], F32, kind="Internal").ap()
    kernels = nc.dram_tensor("kernels", [CH, P - 1 + L], F32, kind="Internal").ap()

    with ExitStack() as ctx:
        def sb(name, shape, dt=F32):
            return ctx.enter_context(nc.sbuf_tensor(name, shape, dt))

        def sem(name):
            return ctx.enter_context(nc.semaphore(name))

        X = sb("X", [P, NB, DM])
        HN = sb("HN", [P, NB, DM])
        B1 = sb("B1", [P, NE * HF])
        B3 = sb("B3", [P, NE * DM])
        raw1 = sb("raw1", [P, 2, HF])
        raw2 = sb("raw2", [P, KF, HF])
        raw3 = sb("raw3", [P, KF, DM])
        ident = sb("ident", [P, P])
        identb = sb("identb", [P, P], BF16)
        anti = sb("anti", [P, P])
        causal = sb("causal", [P, G, P], BF16)
        before = sb("before", [P, P], BF16)
        ones = sb("ones", [P, P], BF16)
        halves = sb("halves", [P, 2])
        gates = sb("gates", [P, 4])
        tg = sb("tg", [P, 4])
        lbias = sb("lbias", [P, NR])
        bgb = sb("bgb", [P, NE])
        wg_sb = sb("wg_sb", [P, 2, NE])
        stats = sb("stats", [P, NB, 6])
        mv = sb("mv", [P, NB, 2])
        ve = sb("ve", [P, NB])
        rstd = sb("rstd", [P, NB])
        minus_half = sb("minus_half", [P, NB])
        zeros = sb("zeros", [P, 2048])
        gl = sb("gl", [P, NB, NE])
        gexp = sb("gexp", [P, NB, NE + 2])
        gsum = sb("gsum", [P, NB])
        grec = sb("grec", [P, NB])
        top8 = sb("top8", [P, NB, 8])
        tidx = sb("tidx", [P, NB, 8], U32)
        wtok = sb("wtok", [P, NB, 2])
        pace = sb("pace", [P, 1])
        gelu_table = sb("gelu_table", [P, 1])
        iota8 = sb("iota8", [P, NE], I32)
        iota_rows = sb("iota_rows", [P, NE], I32)
        iota_rowsf = sb("iota_rowsf", [P, NE])
        iotat = sb("iotat", [P, 32], I32)
        iotatf = sb("iotatf", [P, 32])
        hot = sb("hot", [P, 2, NB, NE])
        chosen = sb("chosen", [P, NB, NE], BF16)
        over = sb("over", [P, NE, NE])
        tiles_of = sb("tiles_of", [P, NE])
        tiles_to = sb("tiles_to", [P, NE])
        onesr = sb("onesr", [P, NE])
        first_tile = sb("first_tile", [P, NE])
        rank = sb("rank", [P, NB, NE])
        slotf = sb("slotf", [P, NB, NE])
        pick = sb("pick", [P, 2, NB, NE])
        slot2f = sb("slot2f", [P, 2, NB])
        slots = sb("slots", [P, 2, NB], I32)
        in_order = sb("in_order", [P, 2, NB])
        wpart = sb("wpart", [P, 2, 2, NB])
        wslot = sb("wslot", [P, 2, NB])
        past = sb("past", [P, NT + 6, NE])
        etf = sb("etf", [P, NT + 6])
        et = sb("et", [P, NT + 6], I32)
        step_f = sb("step_f", [P, NT + 3])
        step_e = sb("step_e", [P, NT + 3], I32)
        tiles_to_i = sb("tiles_to_i", [P, NE], I32)

        s1h = sb("s1h", [P, 2, 2, HF], F32R)
        s1l = sb("s1l", [P, 2, 2, HF], F32R)
        s3h = sb("s3h", [P, 2, KF, DM], F32R)
        s3l = sb("s3l", [P, 2, KF, DM], F32R)
        HT = sb("HT", [P, NB, 2, P])

        with ExitStack() as room:
            def sa(name, shape, dt=F32):
                return room.enter_context(nc.sbuf_tensor(name, shape, dt))

            C = sa("C", [P, NB, DM])
            ct = [sa(f"ct{p}", [P, 2, P]) for p in range(2)]
            va = [sa(f"va{p}", [P, NH, OH]) for p in range(2)]
            xn = [sa(f"xn{p}", [P, DM]) for p in range(2)]
            qh = [[sa(f"qh{p}{o}", [P, 2, P]) for o in range(2)] for p in range(2)]
            pr = [sa(f"pr{p}", [P, G, P]) for p in range(2)]
            pt = [sa(f"pt{p}", [P, G, P]) for p in range(2)]
            rsum = sa("rsum", [P, NH])
            mx = sa("mx", [P, 2, G])
            os_ = sa("os", [P, NG, P])
            on = sa("on", [P, DM])
        s2h = sb("s2h", [P, 2, KF, HF], F32R)
        s2l = sb("s2l", [P, 2, KF, HF], F32R)

        with ExitStack() as room:
            def sl(name, shape, dt=F32):
                return room.enter_context(nc.sbuf_tensor(name, shape, dt))

            LW = sl("LW", [P, 2, NRT + NR + DM])
            LB = sl("LB", [NR, DM])
            sc = sl("sc", [P, NB, NR])
            sg = sl("sg", [P, NB, NRT])
            rep = sl("rep", [P, NB, NR])
            m8 = sl("m8", [P, NB, TOP])
            s8 = sl("s8", [P, NB])
            r8 = sl("r8", [P, NB])
            mg = sl("mg", [P, NB, NR])
            mgT = sl("mgT", [NR, NB, P])
        B2 = sb("B2", [P, NE * HF])

        with ExitStack() as room:
            def sc_(name, shape, dt=F32):
                return room.enter_context(nc.sbuf_tensor(name, shape, dt))

            kp = sc_("kp", [CH, P - 1 + L])
            dcol = sc_("dcol", [CH, 1])
            CT = sc_("CT", [P, 2, NB, P])
            QT = sc_("QT", [P, 2, NB, P])
            us = [sc_(f"us{p}", [P, L]) for p in range(2)]
            kv = [sc_(f"kv{p}", [P, 2, NB, CD * CD]) for p in range(2)]
            z = [sc_(f"z{p}", [P, NB, CD * CD]) for p in range(4)]
            YO = sc_("YO", [P, 2, NB, P])
        xg = [sb(f"xg{p}", [P, DM]) for p in range(2)]
        xh = [sb(f"xh{p}", [P, 2, P], F32R) for p in range(2)]
        xl = [sb(f"xl{p}", [P, 2, P], F32R) for p in range(2)]
        a1 = [sb(f"a1{p}", [P, HF]) for p in range(2)]
        a2 = [sb(f"a2{p}", [P, HF]) for p in range(2)]
        h1h = sb("h1h", [P, KF, P], F32R)
        h1l = sb("h1l", [P, KF, P], F32R)
        h2h = sb("h2h", [P, KF, P], F32R)
        h2l = sb("h2l", [P, KF, P], F32R)
        yt = [sb(f"yt{p}", [P, DM]) for p in range(2)]
        gy = sb("gy", [P, NB, DM])

        bank = [ctx.enter_context(nc.psum_tensor(f"bank{i}", [P, 512], F32)) for i in range(8)]

        loaded_x = [sem("loaded_x0"), sem("loaded_x1")]
        loaded_scales = sem("loaded_scales")
        loaded_c = sem("loaded_c")
        loaded_ct = [sem("loaded_ct0"), sem("loaded_ct1")]
        loaded_small = sem("loaded_small")
        loaded_lora = sem("loaded_lora")
        loaded_ctx_rev = sem("loaded_ctx_rev")
        loaded_bias = sem("loaded_bias")
        loaded_b2 = sem("loaded_b2")
        loaded_u = [sem("loaded_u0"), sem("loaded_u1")]
        loaded_w = [sem("loaded_w1"), sem("loaded_w2"), sem("loaded_w3")]
        cleared = sem("cleared")
        consts = sem("consts")
        pool_step = sem("pool_step")
        dve_step = sem("dve_step")
        tanh_done = sem("tanh_done")
        var_done = sem("var_done")
        rstd_done = sem("rstd_done")
        xn_done = sem("xn_done")
        q_turned = sem("q_turned")
        qh_done = sem("qh_done")
        va_done = sem("va_done")
        scores_done = sem("scores_done")
        max_done = sem("max_done")
        shifted = sem("shifted")
        out_step = sem("out_step")
        probs_done = sem("probs_done")
        p_turned = sem("p_turned")
        pt_done = sem("pt_done")
        pv_done = sem("pv_done")
        os_done = sem("os_done")
        o_turned = sem("o_turned")
        attn_done = sem("attn_done")
        stats_done = sem("stats_done")
        normed = sem("normed")
        h_turned = sem("h_turned")
        ht_done = sem("ht_done")
        routed = sem("routed")
        sig_done = sem("sig_done")
        gated = sem("gated")
        g_turned = sem("g_turned")
        mgt_done = sem("mgt_done")
        ffn_done = sem("ffn_done")
        x2_done = sem("x2_done")
        kv_done = sem("kv_done")
        conv_done = sem("conv_done")
        z_done = sem("z_done")
        yo_done = sem("yo_done")
        y_turned = sem("y_turned")
        x3_done = sem("x3_done")
        logits_done = sem("logits_done")
        gexp_done = sem("gexp_done")
        gshift_done = sem("gshift_done")
        chosen_done = sem("chosen_done")
        counted = sem("counted")
        slots_done = sem("slots_done")
        plan_done = sem("plan_done")
        scattered = [sem("scattered0"), sem("scattered1")]
        loaded_xg = [sem("loaded_xg0"), sem("loaded_xg1")]
        x_turned = sem("x_turned")
        xh_done = sem("xh_done")
        xl_done = sem("xl_done")
        l1_done = sem("l1_done")
        l2_done = sem("l2_done")
        l3_done = sem("l3_done")
        a1_done = sem("a1_done")
        a2_done = sem("a2_done")
        g1_done = sem("g1_done")
        g2_done = sem("g2_done")
        h1_turned = sem("h1_turned")
        h2_turned = sem("h2_turned")
        h1h_done = sem("h1h_done")
        h1l_done = sem("h1l_done")
        h2h_done = sem("h2h_done")
        h2l_done = sem("h2l_done")
        y_done = sem("y_done")
        stored_y = [sem("stored_y0"), sem("stored_y1")]
        kernel_row = sem("kernel_row")
        kernels_stored = sem("kernels_stored")
        split_w = [sem("split_w1"), sem("split_w2"), sem("split_w3")]
        gathered_low = sem("gathered_low")
        lower_added = sem("lower_added")
        gathered = [sem(f"gathered{b}") for b in range(NB)]
        final_done = sem("final_done")
        stored_out = sem("stored_out")

        CREDIT = 8
        by_dve = (xn_done, shifted, attn_done, z_done, a1_done, a2_done, xl_done, h1l_done, h2l_done, y_done, final_done)
        by_act = (os_done, qh_done, probs_done, pt_done, g1_done, g2_done, xh_done, h1h_done, h2h_done)
        by_pe = (o_turned, q_turned, scores_done, p_turned, pv_done, conv_done, l1_done, l2_done, l3_done, x_turned,
                 h1_turned, h2_turned)
        by_pool = (va_done, kv_done)
        ringed = {s.name for s in by_dve + by_act + by_pe + by_pool}

        def of(s, n):
            assert s.name in ringed
            return n + CREDIT

        def give_credit(eng, sems):
            for s in sems:
                eng.sem_inc(s, CREDIT)

        GROUPS = NB * NG

        def run_groups(eng, step):
            for t in range(-NG, NG):
                step(t, t % (2 * NG), t // NG)
            with eng.Fori(0, (NB - 2) // 2) as i:
                for q in range(NG, 3 * NG):
                    step(i * 2 * NG + q, q % (2 * NG), i * 2 + q // NG)
            for t in range(GROUPS - NG, GROUPS + NG + 1):
                step(t, t % (2 * NG), t // NG)

        def within(t, n):
            return not isinstance(t, int) or 0 <= t < n

        FULL = 1
        PAIRS = (NT - 4) // 2

        def run_steps(eng, step):
            for t in range(-4, FULL):
                step(t, t % 2, t // 2)
            with eng.Fori(0, PAIRS) as i:
                for q in range(FULL, FULL + 2):
                    step(i * 2 + q, q % 2, i + q // 2)
            for t in range(FULL + 2 * PAIRS, NT + 1):
                step(t, t % 2, t // 2)

        def exists(t):
            return not isinstance(t, int) or 0 <= t < NT

        block = ctx.enter_context(nc.Block())

        def to_all(ap, n):
            return bass.AP(ap.tensor, ap.offset, [[0, P], [1, n]])

        N_SMALL = 4
        EARLY = NB - 2
        TURNED = (bank[0], bank[3], bank[0], bank[1])
        FIRST = 2
        N_CLEAR = 2 * -(-NT * DM // 2048)

        @block.sync
        def _(sp):
            def context_turned(i, p):
                src = ctx_t[bass.ds(2 * i + p, 1), :, :].rearrange("o (c p) s -> p (o c) s", p=P)
                sp.dma_start(ct[p][:, :, :], src).then_inc(loaded_ct[p], 16)

            sp.dma_start(X[:, 0:FIRST, :], x[0:FIRST].rearrange("b p d -> p b d")).then_inc(loaded_x[0], 16)
            sp.dma_start(halves[:, :], head_halves).then_inc(loaded_scales, 16)
            sp.dma_start(gates[:, 0:2], to_all(g_xattn, 2)).then_inc(loaded_scales, 16)
            sp.dma_start(gates[:, 2:4], to_all(g_ffn, 2)).then_inc(loaded_scales, 16)
            for p in range(2):
                context_turned(0, p)
            sp.dma_start(X[:, FIRST:NB, :], x[FIRST:NB].rearrange("b p d -> p b d")).then_inc(loaded_x[1], 16)
            sp.dma_start(C[:, :, :], ctx_2048.rearrange("b p d -> p b d")).then_inc(loaded_c, 16)
            sp.dma_start(lbias[:, :], to_all(lora_biases, NR)).then_inc(loaded_small, 16)
            sp.dma_start(bgb[:, :], to_all(bg, NE)).then_inc(loaded_small, 16)
            sp.dma_start(wg_sb[:, :, :], wg.rearrange("(c p) n -> p c n", p=P)).then_inc(loaded_small, 16)
            sp.dma_start(LB[:, :], lora_bt).then_inc(loaded_small, 16)
            with sp.Fori(1, NB // 2) as i:
                for p in range(2):
                    sp.wait_ge(scores_done, of(scores_done, i * 2 * NG + (p * NG - NG)))
                    context_turned(i, p)
            sp.dma_start(LW[:, :, :], lora_w.rearrange("(c p) n -> p c n", p=P)).then_inc(loaded_lora, 16)
            for b in range(NB):
                sp.dma_start(CT[:, :, b, :], ctx_t_rev[b].rearrange("(c p) s -> p c s", p=P)).then_inc(loaded_ctx_rev, 16)
            sp.wait_ge(consts, 2)
            sp.dma_start(kp[:, P - 1:P - 1 + L], ssm_kernel).then_inc(kernel_row, 16)
            sp.dma_start(dcol[:, :], ssm_d.rearrange("(h o) -> h o", o=1)).then_inc(kernel_row, 16)
            for sorted_rows in (sorted_x, sorted_y):
                rows = sorted_rows.rearrange("(t p) d -> p t d", p=P)
                for t in range(0, NT, 2048 // DM):
                    n = min(2048 // DM, NT - t)
                    sp.dma_start(rows[:, t:t + n, :], zeros[:, 0:n * DM].rearrange("p (t d) -> p t d", d=DM)).then_inc(cleared, 16)
            sp.dma_start(B1[:, :], to_all(b1, NE * HF)).then_inc(loaded_bias, 16)
            sp.dma_start(B3[:, :], to_all(b3, NE * DM)).then_inc(loaded_bias, 16)
            sp.wait_ge(kernel_row, 33)
            sp.dma_start(kernels, kp[:, :]).then_inc(kernels_stored, 16)
            sp.wait_ge(kernels_stored, 16)
            with sp.Fori(0, CH // 2) as i:
                for p in range(2):
                    sp.wait_ge(conv_done, of(conv_done, i * 4 + (2 * p - 2)))
                    src = bass.AP(kernels.tensor, (2 * i + p) * (P - 1 + L), [[1, P], [1, L]])
                    sp.dma_start(us[p][:, :], src).then_inc(loaded_u[p], 16)
            sp.wait_ge(cleared, 16 * N_CLEAR)
            sp.wait_ge(scattered[0], 16 * NB)

            def step(t, par, half):
                if exists(t + 4):
                    sp.wait_ge(x_turned, of(x_turned, t + 3))
                    if isinstance(t, int) and t + 4 == 1:
                        sp.wait_ge(scattered[1], 16 * NB)
                    sp.dma_start(xg[par][:, :], sorted_x[bass.ts(t + 4, P), :]).then_inc(loaded_xg[par], 16)
                if exists(t - 1):
                    sp.wait_ge(y_done, of(y_done, t))
                    sp.dma_start(sorted_y[bass.ts(t - 1, P), :], yt[1 - par][:, :]).then_inc(stored_y[1 - par], 16)

            run_steps(sp, step)
            for b in range(0, NB, 2):
                sp.wait_ge(final_done, of(final_done, b + 2))
                sp.dma_start(out[b:b + 2].rearrange("b p d -> p b d"), X[:, b:b + 2, :]).then_inc(stored_out, 16)
            for p in range(2):
                sp.wait_ge(stored_y[p], 16 * ((NT + 1 - p) // 2))
            sp.wait_ge(stored_out, 16 * NB // 2)

        @block.gpsimd
        def _(pool):
            give_credit(pool, by_pool)
            n_after = [0]

            def after(ins):
                n_after[0] += 1
                ins.then_inc(pool_step, 1)
                pool.wait_ge(pool_step, n_after[0])

            pool.memset(minus_half[:, :], -0.5)
            pool.memset(onesr[:, :], 1.0)
            pool.memset(ident[:, :], 0.0)
            pool.memset(identb[:, :], 0.0)
            pool.memset(causal[:, :, :], 0.0)
            pool.memset(ones[:, :], 1.0)
            for p in range(2):
                pool.memset(va[p][:, :, HD:OH], 0.0)
            after(pool.memset(before[:, :], 1.0))
            for p in range(2):
                pool.memset(va[p][:, :, HD:HD + 1], 1.0)
            pool.affine_select(out=ident[:, :], in_=ident[:, :], compare_op=ALU.not_equal, fill=1.0, base=0,
                               pattern=[[-1, P]], channel_multiplier=1)
            pool.affine_select(out=identb[:, :], in_=identb[:, :], compare_op=ALU.not_equal, fill=1.0, base=0,
                               pattern=[[-1, P]], channel_multiplier=1)
            pool.affine_select(out=causal[:, :, :], in_=causal[:, :, :], compare_op=ALU.is_ge, fill=MASKED, base=0,
                               pattern=[[0, G], [-1, P]], channel_multiplier=1)
            pool.affine_select(out=before[:, :], in_=before[:, :], compare_op=ALU.is_gt, fill=0.0, base=0,
                               pattern=[[1, P]], channel_multiplier=-1).then_inc(consts, 1)
            norms = [0]

            def inverse_deviation(first, end):
                norms[0] += 1
                pool.wait_ge(var_done, norms[0])
                pool.tensor_tensor(rstd[:, first:end], ve[:, first:end], minus_half[:, first:end], ALU.pow).then_inc(rstd_done, 1)

            def inverse_deviations(first_part=NB // 2):
                inverse_deviation(0, first_part)
                inverse_deviation(first_part, NB)

            inverse_deviation(0, FIRST)

            pool.iota(iota8[:, :], pattern=[[1, NE]], base=0, channel_multiplier=0)
            pool.iota(iota_rows[:, :], pattern=[[P, NE]], base=0, channel_multiplier=0)
            pool.iota(iotat[:, :], pattern=[[1, 32]], base=-3, channel_multiplier=0)
            pool.memset(kp[:, :], 0.0)
            pool.memset(zeros[:, :], 0.0).then_inc(consts, 1)

            for raw, w, loaded in ((raw1, w1, loaded_w[0]), (raw2, w2, loaded_w[1]), (raw3, w3, loaded_w[2])):
                pool.dma_start(raw[:, :, :], w[0].rearrange("(c p) n -> p c n", p=P)).then_inc(loaded, 16)

            parts = ((raw1, s1h, s1l, loaded_w[0], split_w[0]), (raw2, s2h, s2l, loaded_w[1], split_w[1]),
                     (raw3, s3h, s3l, loaded_w[2], split_w[2]))

            def split(e, k):
                raw, high, low, loaded, done = parts[k]
                pool.wait_ge(loaded, (e + 1) * 16)
                pool.tensor_scalar(high[:, e % 2, :, :], raw[:, :, :], 1.0, 1.0, ALU.mult, ALU.mult).then_inc(done, 1)
                pool.wait_ge(done, 2 * e + 1)
                pool.tensor_tensor(low[:, e % 2, :, :], raw[:, :, :], high[:, e % 2, :, :].bitcast(F32),
                                   ALU.subtract).then_inc(done, 1)
                if e + 1 < NE:
                    pool.wait_ge(done, 2 * e + 2)
                    pool.dma_start(raw[:, :, :], (w1, w2, w3)[k][e + 1].rearrange("(c p) n -> p c n", p=P)).then_inc(loaded, 16)

            def values(i, p):
                pool.wait_ge(pv_done, of(pv_done, i * 2 * NG + (p * NG - NG)))
                pool.wait_ge(loaded_c, 16)
                src = C[:, bass.ds(2 * i + p, 1), :].rearrange("p o (h d) -> p (o h) d", d=HD)
                pool.tensor_copy(va[p][:, :, 0:HD], src).then_inc(va_done, 1)

            for p in range(2):
                values(0, p)
            split(0, 0)
            inverse_deviation(FIRST, NB)
            split(0, 2)
            split(1, 0)
            split(1, 2)
            with pool.Fori(1, NB // 2) as i:
                for p in range(2):
                    values(i, p)
            pool.wait_ge(kernel_row, 32)
            pool.tensor_tensor(kp[:, P - 1:P], kp[:, P - 1:P], dcol[:, :], ALU.add).then_inc(kernel_row, 1)
            def products(i, p):
                pool.wait_ge(conv_done, of(conv_done, i * 4 + (2 * p - 2)))
                for c in range(2):
                    kk = CT[:, c, :, bass.ds((2 * i + p) * CD, CD)]
                    o = kv[p][:, c, :, :].rearrange("p b (i j) -> p b i j", j=CD)
                    shape = [P, NB, CD, CD]
                    pool.tensor_tensor(o, kk.unsqueeze(3).broadcast_to(shape), kk.unsqueeze(2).broadcast_to(shape),
                                       ALU.mult).then_inc(kv_done, 1)

            pool.wait_ge(loaded_ctx_rev, 16 * NB)
            for p in range(2):
                products(0, p)
            inverse_deviations(EARLY)
            split(0, 1)
            inverse_deviations()
            with pool.Fori(1, CH // 2) as i:
                for p in range(2):
                    products(i, p)
            split(1, 1)
            inverse_deviations()

            pool.wait_ge(cleared, 16 * N_CLEAR)
            pool.wait_ge(slots_done, 1)
            for k in range(2):
                for b in range(NB):
                    pool.indirect_dma_start(out=sorted_x, out_offset=bass.IndirectOffsetOnAxis(ap=slots[:, k, b:b + 1], axis=0),
                                            in_=HN[:, b, :], in_offset=None).then_inc(scattered[k], 16)

            pool.wait_ge(plan_done, 1)
            for e in range(2, NE):
                last = pool.value_load(tiles_to_i[0:1, e - 2:e - 1], min_val=1, max_val=NT)
                for k, passed in enumerate((l1_done, l2_done, l3_done)):
                    pool.wait_ge(passed, of(passed, last))
                    pool.tensor_tensor(pace[:, :], onesr[:, 0:1], onesr[:, 0:1], ALU.mult)
                    split(e, k)
            def gather(k, dst, done):
                for b in range(NB):
                    pool.indirect_dma_start(out=dst[:, b, :], out_offset=None, in_=sorted_y,
                                            in_offset=bass.IndirectOffsetOnAxis(ap=slots[:, k, b:b + 1], axis=0)
                                            ).then_inc(done[b], 16)

            def tiles_stored(e):
                n = pool.value_load(tiles_to_i[0:1, e:e + 1], min_val=e + 1, max_val=NT)
                for p in range(2):
                    pool.wait_ge(stored_y[p], (n + 1 - p) // 2 * 16)
                    after(pool.tensor_tensor(pace[:, :], onesr[:, 0:1], onesr[:, 0:1], ALU.mult))

            tiles_stored(NE - 2)
            for k in range(2):
                pool.wait_ge(scattered[k], 16 * NB)
            gather(0, HN, [gathered_low] * NB)
            tiles_stored(NE - 1)
            gather(1, gy, gathered)

        @block.tensor
        def _(pe):
            give_credit(pe, by_pe)
            MASKS_AT_START = 6
            TQ, TO, SB, PTB, OB = bank[0], bank[1], bank[2:4], bank[4:6], bank[6:8]
            pe.wait_ge(consts, 1)

            def warm_up(n, o):
                for _ in range(n):
                    pe.matmul(o[:, :], ones[:, :], causal[:, :, :].rearrange("p g k -> p (g k)"), start=True, stop=True)

            warm_up(5, TO)

            def step(t, n, b):
                p, r = n // NG, n % NG
                if within(t, GROUPS):
                    if r == 0:
                        pe.wait_ge(loaded_ct[p], 16 * (b // 2 + 1) if isinstance(b, int) else b * 8 + (16 - 8 * p))
                        pe.wait_ge(qh_done, of(qh_done, b * 2 + 2))
                    pe.wait_ge(shifted, of(shifted, t - 1))
                    o = SB[n % 2]
                    for _ in range(MASKS_AT_START if isinstance(t, int) and t < NG else 1):
                        pe.matmul(o[:, :], identb[:, :], causal[:, :, :].rearrange("p g k -> p (g k)"), start=True, stop=False,
                                  skip_group_check=True)
                    for j in range(G):
                        c, odd = j // 2, j % 2
                        last = pe.matmul(o[:, j * P:(j + 1) * P], qh[p][odd][32 * r:32 * r + 32, c, :],
                                         ct[p][32 * r:32 * r + 32, c, :], start=False, stop=(j == G - 1), skip_group_check=True)
                    last.then_inc(scores_done, 1)
                if within(t - 2, GROUPS):
                    pe.wait_ge(probs_done, of(probs_done, t - 1))
                    pe.wait_ge(pt_done, of(pt_done, t - 3))
                    for j in range(G):
                        last = pe.transpose(PTB[n % 2][:, j * P:(j + 1) * P], pr[n % 2][:, j, :], ident[:, :])
                    last.then_inc(p_turned, 1)
                if within(t - 3, GROUPS):
                    m = (n - 3) % (2 * NG)
                    pm, rm = m // NG, m % NG
                    if rm == 0:
                        pe.wait_ge(va_done, of(va_done, b + 1))
                        pe.wait_ge(os_done, of(os_done, b - 1))
                    pe.wait_ge(pt_done, of(pt_done, t - 2))
                    for j in range(G):
                        h = 8 * (j // 2) + 2 * rm + j % 2
                        last = pe.matmul(OB[pm][32 * j:32 * j + 32, rm * P:(rm + 1) * P], va[pm][:, h, :], pt[m % 2][:, j, :],
                                         start=True, stop=True, skip_group_check=True)
                    last.then_inc(pv_done, 1)
                if r == 1 and within(b + 1, NB):
                    pe.wait_ge(xn_done, of(xn_done, b + 2))
                    pe.wait_ge(qh_done, of(qh_done, b * 2 + 2))
                    for c in range(2):
                        last = pe.transpose(TQ[:, c * P:(c + 1) * P], xn[1 - p][:, c * P:(c + 1) * P], ident[:, :])
                    last.then_inc(q_turned, 1)
                if r == 3 and within(b - 1, NB):
                    pe.wait_ge(os_done, of(os_done, b))
                    pe.wait_ge(attn_done, of(attn_done, b - 1))
                    for k in range(NG):
                        last = pe.transpose(TO[:, k * P:(k + 1) * P], os_[:, k, :], ident[:, :])
                    last.then_inc(o_turned, 1)
                if isinstance(t, int) and t == GROUPS + 1:
                    turn_pair(0, TURNED[0])

            pairs = [0]

            def turn_pair(k, o):
                for b in (2 * k, 2 * k + 1):
                    pe.wait_ge(normed, pairs[0] * 2 + b % 2 + 1)
                    for c in range(2):
                        last = pe.transpose(o[:, (2 * (b % 2) + c) * P:(2 * (b % 2) + c + 1) * P],
                                            HN[:, b, c * P:(c + 1) * P], ident[:, :])
                pairs[0] += 1
                last.then_inc(h_turned, 1)

            def turn_norm(banks):
                for k in range(NB // 2):
                    if k >= 2:
                        pe.wait_ge(ht_done, pairs[0] - 1)
                    turn_pair(k, banks[k % 2])

            run_groups(pe, step)

            pe.wait_ge(loaded_lora, 16)
            pe.wait_ge(loaded_small, 16 * N_SMALL)
            NW = NRT + NR

            def route(b):
                if b % 2 == 0:
                    pe.wait_ge(ht_done, b // 2 + 1)
                for c in range(2):
                    last = pe.matmul(bank[2 + b // 4][:, (b % 4) * P:(b % 4) * P + NW], HT[:, b, c, :], LW[:, c, 0:NW],
                                     start=(c == 0), stop=(c == 1), skip_group_check=True)
                if b % 4 == 3:
                    last.then_inc(routed, 1)

            def base(b):
                o = bank[4 + b // 2][:, (b % 2) * DM:(b % 2 + 1) * DM]
                for c in range(2):
                    pe.matmul(o, HT[:, b, c, :], LW[:, c, NW:NW + DM], start=(b % 2 == 0 and c == 0), stop=False,
                              skip_group_check=True)

            pe.wait_ge(ht_done, 1)
            turn_pair(1, TURNED[1])
            turn_pair(2, TURNED[2])
            for b in range(EARLY):
                route(b)
            base(0)
            turn_pair(3, TURNED[3])
            for b in (1, 2):
                base(b)
            for b in range(EARLY, NB):
                route(b)
            for b in range(3, NB):
                base(b)
            warm_up(10, bank[0])
            for b in range(NB):
                pe.wait_ge(gated, b + 1)
                last = pe.transpose(bank[b // 4][0:NR, (b % 4) * P:(b % 4 + 1) * P], mg[:, b, :], ident[:, :])
                if b % 4 == 3:
                    last.then_inc(g_turned, 1)
            for b in range(NB):
                o = bank[4 + b // 2][:, (b % 2) * DM:(b % 2 + 1) * DM]
                if b % 4 == 0:
                    pe.wait_ge(mgt_done, b // 4 + 1)
                last = pe.matmul(o, mgT[:, b, :], LB[:, :], start=False, stop=True, skip_group_check=True)
                if b % 2:
                    last.then_inc(ffn_done, 1)

            YB = bank[2:6]

            def convolve(i, p):
                pe.wait_ge(loaded_u[p], i * 16 + 16)
                for c in range(2):
                    n = 2 * p + c
                    pe.wait_ge(kv_done, of(kv_done, i * 4 + (n + 1)))
                    pe.wait_ge(z_done, of(z_done, i * 4 + (n - 3)))
                    o = YB[n][:, :]
                    rhs = kv[p][:, :, :, :].rearrange("p c b k -> p c (b k)")
                    if c == 0:
                        last = pe.matmul(o, us[p][:, 0:P], rhs[:, 0, :], start=True, stop=True)
                    else:
                        pe.matmul(o, us[p][:, P:2 * P], rhs[:, 0, :], start=True, stop=False)
                        last = pe.matmul(o, us[p][:, 0:P], rhs[:, 1, :], start=False, stop=True)
                    last.then_inc(conv_done, 1)

            convolve(0, 0)
            pe.wait_ge(x2_done, NB // 2)
            convolve(0, 1)
            turn_norm(bank[0:2])
            with pe.Fori(1, CH // 2) as i:
                for p in range(2):
                    convolve(i, p)
            pe.wait_ge(yo_done, 1)
            for b in range(NB):
                if b >= 4:
                    pe.wait_ge(x3_done, b - 3)
                for c in range(2):
                    last = pe.transpose(bank[b % 4][:, c * P:(c + 1) * P], YO[:, c, b, :], ident[:, :])
                last.then_inc(y_turned, 1)

            warm_up(24, bank[7])
            def logits(k):
                pe.wait_ge(ht_done, NB + k + 1)
                for b in (2 * k, 2 * k + 1):
                    for c in range(2):
                        last = pe.matmul(bank[6][:, b * NE:(b + 1) * NE], HT[:, b, c, :], wg_sb[:, c, :],
                                         start=(c == 0), stop=(c == 1), skip_group_check=True)
                return last

            turn_pair(0, bank[4])
            turn_pair(1, bank[5])
            logits(0)
            turn_pair(2, bank[4])
            logits(1)
            turn_pair(3, bank[5])
            logits(2)
            logits(3).then_inc(logits_done, 1)
            pe.wait_ge(chosen_done, 1)
            pe.matmul(bank[7][:, 0:NB * NE], before[:, :], chosen[:, :, :].rearrange("p b e -> p (b e)"), start=True,
                      stop=False, skip_group_check=True)
            for b in range(NB - 1):
                for b2 in range(b + 1, NB):
                    pe.matmul(bank[7][:, b2 * NE:(b2 + 1) * NE], ones[:, :], chosen[:, b, :],
                              start=False, stop=(b == NB - 2), skip_group_check=True)
            for b in range(NB):
                last = pe.matmul(bank[4][:, 0:NE], ones[:, :], chosen[:, b, :], start=(b == 0), stop=(b == NB - 1))
            last.then_inc(counted, 1)

            pe.wait_ge(plan_done, 1)

            def experts(t):
                v = pe.value_load(step_e[0:1, bass.ds(t + 2, 1)], min_val=0, max_val=NE ** 3 - 1)
                return {-1: v % NE, 1: (v // NE) % NE, 2: v // (NE * NE)}

            def layer(e, k, o, high, low, w_high, w_low, n_k, done):
                pe.wait_ge(split_w[k], e * 2 + 2)
                for j in range(n_k):
                    for m, (a, w) in enumerate(((high, w_high), (high, w_low), (low, w_high))):
                        last = pe.matmul(o, a[:, j, :], w[:, bass.ds(e % 2, 1), j, :].rearrange("p o n -> p (o n)"),
                                         start=(j == 0 and m == 0), stop=(j == n_k - 1 and m == 2))
                last.then_inc(done, 1)

            def turn(o, src, n_k, done):
                for j in range(n_k):
                    last = pe.transpose(o[:, j * P:(j + 1) * P], src[:, j * P:(j + 1) * P], ident[:, :])
                last.then_inc(done, 1)

            def step(t, par, half):
                e = experts(t) if not isinstance(t, int) or t >= -2 else {}
                if exists(t - 1):
                    pe.wait_ge(h2h_done, of(h2h_done, t))
                    pe.wait_ge(h2l_done, of(h2l_done, t))
                    pe.wait_ge(y_done, of(y_done, t - 1))
                    layer(e[-1], 2, bank[5][:, 0:DM], h2h, h2l, s3h, s3l, KF, l3_done)
                if exists(t + 1):
                    pe.wait_ge(g1_done, of(g1_done, t + 2))
                    pe.wait_ge(h1l_done, of(h1l_done, t + 1))
                    turn(bank[1], a1[1 - par], KF, h1_turned)
                if exists(t):
                    pe.wait_ge(g2_done, of(g2_done, t + 1))
                    pe.wait_ge(h2l_done, of(h2l_done, t))
                    turn(bank[2], a2[par], KF, h2_turned)
                if exists(t + 2):
                    pe.wait_ge(xh_done, of(xh_done, t + 3))
                    pe.wait_ge(xl_done, of(xl_done, t + 3))
                    pe.wait_ge(a1_done, of(a1_done, t + 2))
                    layer(e[2], 0, bank[3][:, :], xh[par], xl[par], s1h, s1l, 2, l1_done)
                if isinstance(t, int) and t == -2:
                    warm_up(8, bank[5])
                if exists(t + 3):
                    pe.wait_ge(loaded_xg[1 - par], 16 * (half + (par + 3) // 2 + 1))
                    pe.wait_ge(xl_done, of(xl_done, t + 3))
                    turn(bank[0], xg[1 - par], 2, x_turned)
                if exists(t + 1):
                    pe.wait_ge(h1h_done, of(h1h_done, t + 2))
                    pe.wait_ge(h1l_done, of(h1l_done, t + 2))
                    pe.wait_ge(a2_done, of(a2_done, t + 1))
                    layer(e[1], 1, bank[4][:, :], h1h, h1l, s2h, s2l, KF, l2_done)

            run_steps(pe, step)

        @block.scalar
        def _(act):
            give_credit(act, by_act)
            act.wait_ge(loaded_scales, 48)
            act.activation(tg[:, :], gates[:, :], ACT.Tanh).then_inc(tanh_done, 1)
            def step(t, n, b):
                p, r = n // NG, n % NG
                if within(t - 2, GROUPS):
                    act.wait_ge(p_turned, of(p_turned, t - 1))
                    act.wait_ge(pv_done, of(pv_done, t - 3))
                    act.activation(pt[n % 2][:, :, :], bank[4 + n % 2][:, :].rearrange("p (g s) -> p g s", g=G),
                                   ACT.Copy).then_inc(pt_done, 1)
                if r == 2 and within(b - 1, NB):
                    act.wait_ge(pv_done, of(pv_done, b * NG))
                    act.wait_ge(o_turned, of(o_turned, b - 1))
                    act.activation(os_[:, :, :], bank[6 + (1 - p)][:, :].rearrange("p (r s) -> p r s", r=NG),
                                   ACT.Copy).then_inc(os_done, 1)
                if within(t, GROUPS):
                    act.wait_ge(shifted, of(shifted, t + 1))
                    act.activation(pr[n % 2][:, :, :], pr[n % 2][:, :, :], ACT.Exp).then_inc(probs_done, 1)
                if r == 1 and within(b + 1, NB):
                    act.wait_ge(q_turned, of(q_turned, b + 2))
                    act.wait_ge(scores_done, of(scores_done, b * NG))
                    for odd in range(2):
                        act.activation(qh[1 - p][odd][:, :, :], bank[0][:, 0:DM].rearrange("p (c s) -> p c s", c=2), ACT.Copy,
                                       scale=halves[:, odd:odd + 1]).then_inc(qh_done, 1)
                if isinstance(t, int) and t == GROUPS + 1:
                    copy_pair(TURNED[0], HT[:, 0:2, :, :])

            copied = [0]

            def copy_pair(src, dst):
                copied[0] += 1
                act.wait_ge(h_turned, copied[0])
                act.activation(dst, src[:, :].rearrange("p (b c s) -> p b c s", b=2, c=2), ACT.Copy).then_inc(ht_done, 1)

            def copy_turned(banks, dst):
                for k in range(NB // 2):
                    copy_pair(banks[k % 2], dst(k))

            run_groups(act, step)

            for k in range(1, NB // 2):
                copy_pair(TURNED[k], HT[:, 2 * k:2 * k + 2, :, :])
            for k in range(2):
                act.wait_ge(routed, k + 1)
                act.activation(sg[:, 4 * k:4 * k + 4, :], bank[2 + k][:, :].rearrange("p (b n) -> p b n", b=4)[:, :, 0:NRT],
                               ACT.Exp, scale=-1.0).then_inc(sig_done, 1)
            for k in range(2):
                act.wait_ge(g_turned, k + 1)
                act.activation(mgT[:, 4 * k:4 * k + 4, :], bank[k][0:NR, :].rearrange("p (b s) -> p b s", b=4),
                               ACT.Copy).then_inc(mgt_done, 1)
            copy_turned(bank[0:2], lambda k: QT[:, :, 2 * k:2 * k + 2, :].rearrange("p c b s -> p b c s"))
            act.wait_ge(x2_done, NB)
            act.dma_start(B2[:, :], to_all(b2, NE * HF)).then_inc(loaded_b2, 16)
            copy_turned(bank[4:6], lambda k: HT[:, 2 * k:2 * k + 2, :, :])
            act.wait_ge(gshift_done, 1)
            act.activation(gexp[:, :, :], gexp[:, :, :], ACT.Exp).then_inc(gexp_done, 1)
            act.activation(gelu_table[:, :], ones[:, 0:1], ACT.Gelu)

            def step(t, par, half):
                if exists(t):
                    act.wait_ge(a2_done, of(a2_done, t + 1))
                    act.activation(a2[par][:, :], a2[par][:, :], ACT.Gelu).then_inc(g2_done, 1)
                if exists(t + 1):
                    act.wait_ge(h1_turned, of(h1_turned, t + 2))
                    act.wait_ge(l2_done, of(l2_done, t + 1))
                    act.activation(h1h[:, :, :], bank[1][:, :].rearrange("p (k s) -> p k s", k=KF), ACT.Copy).then_inc(h1h_done, 1)
                if exists(t):
                    act.wait_ge(h2_turned, of(h2_turned, t + 1))
                    act.wait_ge(l3_done, of(l3_done, t))
                    act.activation(h2h[:, :, :], bank[2][:, :].rearrange("p (k s) -> p k s", k=KF), ACT.Copy).then_inc(h2h_done, 1)
                if exists(t + 2):
                    act.wait_ge(a1_done, of(a1_done, t + 3))
                    act.activation(a1[par][:, :], a1[par][:, :], ACT.Gelu).then_inc(g1_done, 1)
                if exists(t + 3):
                    act.wait_ge(x_turned, of(x_turned, t + 4))
                    act.wait_ge(l1_done, of(l1_done, t + 2))
                    act.activation(xh[1 - par][:, :, :], bank[0][:, 0:DM].rearrange("p (c s) -> p c s", c=2),
                                   ACT.Copy).then_inc(xh_done, 1)

            run_steps(act, step)

        @block.vector
        def _(dve):
            give_credit(dve, by_dve)
            n_after = [0]

            def after(ins):
                n_after[0] += 1
                ins.then_inc(dve_step, 1)
                dve.wait_ge(dve_step, n_after[0])

            norms = [0]

            halves_of_batches = [range(0, NB // 2), range(NB // 2, NB)]

            def add_up(batches):
                for b in batches:
                    ins = dve.bn_aggr(mv[:, b, :], stats[:, b, :])
                after(ins)
                some = slice(batches[0], batches[-1] + 1)
                dve.tensor_scalar(ve[:, some], mv[:, some, 1], EPS, None, ALU.add).then_inc(var_done, 1)

            def await_deviations():
                norms[0] += 1
                dve.wait_ge(rstd_done, norms[0])

            def norm(batches):
                for b in batches:
                    dve.tensor_scalar(HN[:, b, :], X[:, b, :], mv[:, b, 0:1], rstd[:, b:b + 1], ALU.subtract,
                                      ALU.mult).then_inc(normed, 1)

            def update_and_norm(update, updated):
                for batches in halves_of_batches:
                    for b in batches:
                        update(b)
                    dve.wait_ge(updated, batches[-1] + 1)
                    for b in batches:
                        ins = dve.bn_stats(stats[:, b, :], X[:, b, :])
                    after(ins)
                    add_up(batches)
                for batches in halves_of_batches:
                    await_deviations()
                    norm(batches)

            def statistics(batches):
                for b in batches:
                    ins = dve.bn_stats(stats[:, b, :], X[:, b, :])
                after(ins)

            dve.wait_ge(loaded_x[0], 16)
            statistics(range(FIRST))
            add_up(range(FIRST))
            await_deviations()

            def step(t, n, b):
                p, r = n // NG, n % NG
                if r == 0 and within(b + 1, NB):
                    dve.wait_ge(q_turned, of(q_turned, b))
                    nb = b + 1
                    dve.tensor_scalar(xn[1 - p][:, :], X[:, bass.ds(nb, 1), :].rearrange("p o d -> p (o d)"),
                                      mv[:, bass.ds(nb, 1), 0:1].rearrange("p o d -> p (o d)"), rstd[:, bass.ds(nb, 1)],
                                      ALU.subtract, ALU.mult).then_inc(xn_done, 1)
                if within(t, GROUPS):
                    dve.wait_ge(scores_done, of(scores_done, t + 1))
                    sg_ = bank[2 + n % 2][:, :].rearrange("p (g k) -> p g k", g=G)
                    dve.tensor_reduce(mx[:, n % 2, :], sg_, AX.X, ALU.max).then_inc(max_done, 1)
                    dve.wait_ge(max_done, t + 1)
                    dve.wait_ge(p_turned, of(p_turned, t - 1))
                    dve.tensor_tensor(pr[n % 2][:, :, :], sg_, mx[:, n % 2, :].unsqueeze(2).broadcast_to([P, G, P]),
                                      ALU.subtract).then_inc(shifted, 1)
                if isinstance(t, int) and 0 <= t < NG - 1:
                    dve.wait_ge(loaded_x[1], 16)
                    statistics(range(FIRST + 2 * t, FIRST + 2 * t + 2))
                    if t == NG - 2:
                        add_up(range(FIRST, NB))
                if isinstance(t, int) and t == NG - 1:
                    await_deviations()
                if r == 3 and within(b - 1, NB):
                    def then(k, ins):
                        ins.then_inc(out_step, 1)
                        dve.wait_ge(out_step, (b - 1) * 2 + k)

                    dve.wait_ge(o_turned, of(o_turned, b))
                    o = bank[1][:, :].rearrange("p (r c o d) -> p c r o d", r=NG, c=2, o=2)
                    then(1, dve.reciprocal(rsum[:, :].rearrange("p (c r o) -> p c r o", c=2, r=NG), o[:, :, :, :, HD]))
                    for c in range(2):
                        ins = dve.tensor_tensor(on[:, c * P:(c + 1) * P].rearrange("p (r o d) -> p r o d", r=NG, d=HD),
                                                o[:, c, :, :, 0:HD],
                                                rsum[:, c * 8:c * 8 + 8].rearrange("p (r o) -> p r o", r=NG).unsqueeze(3).broadcast_to([P, NG, 2, HD]),
                                                ALU.mult)
                    then(2, ins)
                    xb = X[:, bass.ds(b - 1, 1), :].rearrange("p o d -> p (o d)")
                    dve.scalar_tensor_tensor(out=xb, in0=on[:, :], scalar=tg[:, 0:1], in1=xb, op0=ALU.mult,
                                             op1=ALU.add).then_inc(attn_done, 1)
                    dve.wait_ge(attn_done, of(attn_done, b))
                    dve.bn_stats(stats[:, bass.ds(b - 1, 1), :].rearrange("p o d -> p (o d)"), xb).then_inc(stats_done, 1)

                if isinstance(t, int) and t == GROUPS - NG:
                    add_up(range(EARLY))
                if isinstance(t, int) and t == GROUPS - NG + 1:
                    await_deviations()
                    norm(range(0, 2))
                if isinstance(t, int) and t == GROUPS:
                    norm(range(2, EARLY))

            run_groups(dve, step)
            after(dve.tensor_copy(iota_rowsf[:, :], iota_rows[:, :]))
            dve.tensor_scalar(iota_rowsf[:, 0:1], iota_rowsf[:, 0:1], 1.0, None, ALU.subtract)
            after(dve.tensor_copy(iotatf[:, :], iotat[:, :]))
            dve.wait_ge(attn_done, of(attn_done, NB))

            dve.wait_ge(stats_done, NB)
            add_up(range(EARLY, NB))
            await_deviations()
            norm(range(EARLY, NB))
            for k, batches in enumerate(halves_of_batches):
                some = slice(batches[0], batches[-1] + 1)
                dve.wait_ge(sig_done, k + 1)
                after(dve.tensor_scalar(sg[:, some, :], sg[:, some, :], 1.0, None, ALU.add))
                ins = dve.reciprocal(sg[:, some, :], sg[:, some, :])
            after(ins)
            shape = [P, NB, NRT, 2]
            after(dve.tensor_tensor(sc[:, :, :].rearrange("p b (n r) -> p b n r", r=2), sg[:, :, :].unsqueeze(3).broadcast_to(shape),
                                    lbias[:, :].rearrange("p (n r) -> p n r", r=2).unsqueeze(1).broadcast_to(shape), ALU.add))
            for b in range(NB):
                ins = dve.max(m8[:, b, :], sc[:, b, :])
            after(ins)
            dve.tensor_reduce(s8[:, :], m8[:, :, :], AX.X, ALU.add)
            for b in range(NB):
                ins = dve.match_replace(rep[:, b, :], m8[:, b, :], sc[:, b, :], TAKEN)
            after(ins)
            after(dve.reciprocal(r8[:, :], s8[:, :]))
            dve.tensor_scalar(r8[:, :], r8[:, :], float(TOP * SCALING), None, ALU.mult)
            after(dve.scalar_tensor_tensor(out=rep[:, :, :], in0=rep[:, :, :], scalar=TAKEN, in1=sc[:, :, :],
                                           op0=ALU.is_equal, op1=ALU.mult))
            for b in range(NB):
                mid = bank[2 + b // 4][:, (b % 4) * P + NRT:(b % 4) * P + NRT + NR]
                dve.scalar_tensor_tensor(out=mg[:, b, :], in0=rep[:, b, :], scalar=r8[:, b:b + 1], in1=mid,
                                         op0=ALU.mult, op1=ALU.mult).then_inc(gated, 1)

            def add_ffn(b):
                if b % 2 == 0:
                    dve.wait_ge(ffn_done, b // 2 + 1)
                dve.scalar_tensor_tensor(out=X[:, b, :], in0=bank[4 + b // 2][:, (b % 2) * DM:(b % 2 + 1) * DM],
                                         scalar=tg[:, 2:3], in1=X[:, b, :], op0=ALU.mult, op1=ALU.add).then_inc(x2_done, 1)

            update_and_norm(add_ffn, x2_done)
            dve.wait_ge(ht_done, 8)
            first_sum = n_after[0]
            by_ij = [P, NB, CD, CD]
            z_ij = [zz[:, :, :].rearrange("p b (i j) -> p b i j", j=CD) for zz in z]

            def weigh(i, n):
                p, c = n // 2, n % 2
                cols = bass.ds((2 * i + p) * CD, CD)
                dve.wait_ge(conv_done, of(conv_done, i * 4 + (n + 1)))
                dve.wait_ge(dve_step, i * 4 + (first_sum + n - 3))
                dve.tensor_tensor(z_ij[n], bank[2 + n][:, :].rearrange("p (b i j) -> p b i j", b=NB, j=CD),
                                  QT[:, c, :, cols].unsqueeze(3).broadcast_to(by_ij), ALU.mult).then_inc(z_done, 1)

            def sum_up(i, n):
                p, c = n // 2, n % 2
                cols = bass.ds((2 * i + p) * CD, CD)
                dve.wait_ge(z_done, of(z_done, i * 4 + (n + 1)))
                dve.tensor_reduce(YO[:, c, :, cols], z_ij[n].rearrange("p b i j -> p b j i"), AX.X, ALU.add).then_inc(dve_step, 1)

            weigh(0, 0)
            with dve.Fori(0, CH // 2 - 1) as i:
                for n in range(4):
                    weigh(i + (n + 1) // 4, (n + 1) % 4)
                    sum_up(i, n)
            last_pair = CH // 2 - 1
            for n in range(4):
                if n < 3:
                    weigh(last_pair, n + 1)
                sum_up(last_pair, n)
            n_after[0] = first_sum + 2 * CH
            dve.wait_ge(dve_step, n_after[0])
            dve.sem_inc(yo_done, 1)

            def add_hyena(b):
                dve.wait_ge(y_turned, b + 1)
                dve.scalar_tensor_tensor(out=X[:, b, :], in0=bank[b % 4][:, 0:DM], scalar=tg[:, 1:2], in1=X[:, b, :],
                                         op0=ALU.mult, op1=ALU.add).then_inc(x3_done, 1)

            update_and_norm(add_hyena, x3_done)
            dve.wait_ge(logits_done, 1)
            by_e = [P, NB, NE]
            after(dve.tensor_tensor(gl[:, :, :], bank[6][:, 0:NB * NE].rearrange("p (b e) -> p b e", e=NE),
                                    bgb[:, :].unsqueeze(1).broadcast_to(by_e), ALU.add))
            for b in range(NB):
                ins = dve.max(top8[:, b, :], gl[:, b, :])
            after(ins)
            for b in range(NB):
                ins = dve.max_index(tidx[:, b, :], top8[:, b, :], gl[:, b, :])
            after(ins)
            by_ke = [P, 2, NB, NE]
            after(dve.tensor_tensor(hot[:, :, :, :], iota8[:, :].unsqueeze(1).unsqueeze(1).broadcast_to(by_ke),
                                    tidx[:, :, 0:2].rearrange("p b k -> p k b").unsqueeze(3).broadcast_to(by_ke), ALU.is_equal))
            dve.tensor_tensor(chosen[:, :, :], hot[:, 0, :, :], hot[:, 1, :, :], ALU.add).then_inc(chosen_done, 1)
            largest = top8[:, :, 0:1]
            dve.tensor_tensor(gexp[:, :, 0:NE], gl[:, :, :], largest.broadcast_to(by_e), ALU.subtract)
            dve.tensor_tensor(gexp[:, :, NE:NE + 2], top8[:, :, 0:2], largest.broadcast_to([P, NB, 2]),
                              ALU.subtract).then_inc(gshift_done, 1)
            dve.wait_ge(counted, 1)
            e_by_j = [P, NE, NE]
            after(dve.tensor_tensor(over[:, :, :], bank[4][:, 0:NE].unsqueeze(2).broadcast_to(e_by_j),
                                    iota_rowsf[:, :].unsqueeze(1).broadcast_to(e_by_j), ALU.is_gt))
            after(dve.tensor_reduce(tiles_of[:, :], over[:, :, :], AX.X, ALU.add))
            after(dve.tensor_tensor_scan(tiles_to[:, :], onesr[:, :], tiles_of[:, :], 0.0, ALU.mult, ALU.add))
            after(dve.tensor_tensor(first_tile[:, :], tiles_to[:, :], tiles_of[:, :], ALU.subtract))
            after(dve.scalar_tensor_tensor(out=slotf[:, :, :], in0=first_tile[:, :].unsqueeze(1).broadcast_to(by_e), scalar=float(P),
                                           in1=bank[7][:, 0:NB * NE].rearrange("p (b e) -> p b e", e=NE), op0=ALU.mult, op1=ALU.add))
            after(dve.tensor_tensor(pick[:, :, :, :], hot[:, :, :, :], slotf[:, :, :].unsqueeze(1).broadcast_to(by_ke), ALU.mult))
            after(dve.tensor_reduce(slot2f[:, :, :], pick[:, :, :, :], AX.X, ALU.add))
            dve.tensor_tensor(slots[:, 0, :], slot2f[:, 0, :], slot2f[:, 1, :], ALU.min)
            dve.tensor_tensor(slots[:, 1, :], slot2f[:, 0, :], slot2f[:, 1, :], ALU.max).then_inc(slots_done, 1)
            t_by_e = [P, NT + 6, NE - 1]
            after(dve.tensor_tensor(past[:, :, 0:NE - 1], iotatf[:, 0:NT + 6].unsqueeze(2).broadcast_to(t_by_e),
                                    tiles_to[:, 0:NE - 1].unsqueeze(1).broadcast_to(t_by_e), ALU.is_ge))
            after(dve.tensor_reduce(etf[:, :], past[:, :, 0:NE - 1], AX.X, ALU.add))
            dve.tensor_copy(tiles_to_i[:, :], tiles_to[:, :])
            dve.tensor_copy(et[:, :], etf[:, :])
            after(dve.scalar_tensor_tensor(out=step_f[:, :], in0=etf[:, 3:NT + 6], scalar=float(NE), in1=etf[:, 2:NT + 5],
                                           op0=ALU.mult, op1=ALU.add))
            after(dve.scalar_tensor_tensor(out=step_f[:, :], in0=step_f[:, :], scalar=float(NE), in1=etf[:, 0:NT + 3],
                                           op0=ALU.mult, op1=ALU.add))
            dve.tensor_copy(step_e[:, :], step_f[:, :]).then_inc(plan_done, 1)
            dve.wait_ge(plan_done, 1)
            dve.wait_ge(gexp_done, 1)
            after(dve.tensor_reduce(gsum[:, :], gexp[:, :, 0:NE], AX.X, ALU.add))
            after(dve.reciprocal(grec[:, :], gsum[:, :]))
            after(dve.tensor_tensor(wtok[:, :, :], gexp[:, :, NE:NE + 2], grec[:, :].unsqueeze(2).broadcast_to([P, NB, 2]), ALU.mult))
            after(dve.tensor_scalar(wtok[:, :, :], wtok[:, :, :], tg[:, 3:4], None, ALU.mult))
            dve.tensor_tensor(in_order[:, 0, :], slot2f[:, 0, :], slot2f[:, 1, :], ALU.is_lt)
            after(dve.tensor_tensor(in_order[:, 1, :], slot2f[:, 0, :], slot2f[:, 1, :], ALU.is_ge))
            for k in range(2):
                for c in range(2):
                    ins = dve.tensor_tensor(wpart[:, k, c, :], in_order[:, (k + c) % 2, :], wtok[:, :, c], ALU.mult)
            after(ins)
            after(dve.tensor_tensor(wslot[:, :, :], wpart[:, :, 0, :], wpart[:, :, 1, :], ALU.add))
            dve.wait_ge(loaded_bias, 32)
            dve.wait_ge(loaded_b2, 16)

            def bias_at(t, table, n):
                e = dve.value_load(et[0:1, bass.ds(t + 3, 1)], min_val=0, max_val=NE - 1)
                return table[:, bass.ds(e * n, n)]

            def low(dst, src, high_part, done):
                dve.tensor_tensor(dst, src, high_part.bitcast(F32), ALU.subtract).then_inc(done, 1)

            def add_lower(batches):
                dve.wait_ge(gathered_low, 16 * NB)
                for b in batches:
                    dve.scalar_tensor_tensor(out=X[:, b, :], in0=HN[:, b, :], scalar=wslot[:, 0, b:b + 1], in1=X[:, b, :],
                                             op0=ALU.mult, op1=ALU.add).then_inc(lower_added, 1)

            def step(t, par, half):
                if exists(t):
                    bias = bias_at(t, B2, HF)
                    dve.wait_ge(l2_done, of(l2_done, t + 1))
                    dve.wait_ge(h2_turned, of(h2_turned, t - 1))
                    dve.tensor_tensor(a2[par][:, :], bank[4][:, :], bias, ALU.add).then_inc(a2_done, 1)
                if exists(t - 1):
                    bias = bias_at(t - 1, B3, DM)
                    dve.wait_ge(l3_done, of(l3_done, t))
                    dve.wait_ge(stored_y[1 - par], 16 * (half + (par - 1) // 2))
                    dve.tensor_tensor(yt[1 - par][:, :], bank[5][:, 0:DM], bias, ALU.add).then_inc(y_done, 1)
                if isinstance(t, int) and t == NT - 1:
                    add_lower(halves_of_batches[0])
                if exists(t + 1):
                    dve.wait_ge(h1h_done, of(h1h_done, t + 2))
                    dve.wait_ge(l2_done, of(l2_done, t + 1))
                    low(h1l[:, :, :], bank[1][:, :].rearrange("p (k s) -> p k s", k=KF), h1h[:, :, :], h1l_done)
                if exists(t):
                    dve.wait_ge(h2h_done, of(h2h_done, t + 1))
                    dve.wait_ge(l3_done, of(l3_done, t))
                    low(h2l[:, :, :], bank[2][:, :].rearrange("p (k s) -> p k s", k=KF), h2h[:, :, :], h2l_done)
                if isinstance(t, int) and t == NT - 1:
                    add_lower(halves_of_batches[1])
                if exists(t + 2):
                    bias = bias_at(t + 2, B1, HF)
                    dve.wait_ge(l1_done, of(l1_done, t + 3))
                    dve.wait_ge(h1_turned, of(h1_turned, t + 1))
                    dve.tensor_tensor(a1[par][:, :], bank[3][:, :], bias, ALU.add).then_inc(a1_done, 1)
                if exists(t + 3):
                    dve.wait_ge(xh_done, of(xh_done, t + 4))
                    dve.wait_ge(l1_done, of(l1_done, t + 2))
                    low(xl[1 - par][:, :, :], bank[0][:, 0:DM].rearrange("p (c s) -> p c s", c=2), xh[1 - par][:, :, :], xl_done)

            run_steps(dve, step)
            dve.wait_ge(lower_added, NB)
            for b in range(NB):
                dve.wait_ge(gathered[b], 16)
                dve.scalar_tensor_tensor(out=X[:, b, :], in0=gy[:, b, :], scalar=wslot[:, 1, b:b + 1], in1=X[:, b, :],
                                         op0=ALU.mult, op1=ALU.add).then_inc(final_done, 1)


def kernel(**inputs):
    import numpy as np
    import concourse.bacc as bacc
    from concourse.bass_utils import run_bass_kernel_spmd

    a = {k: np.asarray(v) for k, v in inputs.items()}
    ctx = a["ctx_2048"]
    nb, s, d = ctx.shape
    ctx_t = ctx.transpose(0, 2, 1)
    halves = np.zeros((128, 2), np.float32)
    halves[np.arange(128) % 32 < 16, 0] = 0.25
    halves[np.arange(128) % 32 >= 16, 1] = 0.25
    arrays = {
        "x": a["x"],
        "ctx_2048": ctx,
        "ctx_t": ctx_t,
        "ctx_t_rev": ctx_t.reshape(nb, d // 128, 128, s)[:, :, ::-1].reshape(nb, d, s),
        "g_xattn": a["g_xattn"],
        "g_ffn": a["g_ffn"],
        "lora_w": np.concatenate([a["L0_ffn_router_W"].T, a["L0_ffn_A"].T, a["L0_ffn_base_W"].T], axis=1),
        "lora_bt": a["L0_ffn_B"].T,
        "lora_biases": a["L0_ffn_biases"],
        "ssm_kernel": a["L1_xattn_ssm_kernel"],
        "ssm_d": a["L1_xattn_D"],
        "w1": a["L1_ffn_W1"],
        "w2": a["L1_ffn_W2"],
        "w3": a["L1_ffn_W3"],
        "b1": a["L1_ffn_b1"],
        "b2": a["L1_ffn_b2"],
        "b3": a["L1_ffn_b3"],
        "wg": a["L1_ffn_Wg"],
        "bg": a["L1_ffn_bg"],
        "head_halves": halves,
    }
    nc = bacc.Bacc("TRN2", target_bir_lowering=False, num_devices=1)
    feed, args = {}, {}
    for name, v in arrays.items():
        v = np.ascontiguousarray(v)
        feed[f"in_{name}"] = v
        args[name] = nc.dram_tensor(f"in_{name}", v.shape, mybir.dt.from_np(v.dtype), kind="ExternalInput").ap()
    result = nc.dram_tensor("result", a["x"].shape, mybir.dt.float32, kind="ExternalOutput").ap()
    flamingo_two_layers(nc, out=result, **args)
    r = run_bass_kernel_spmd(nc, [feed], core_ids=[0])
    return r.results[0]["result"]
```
